# Optimizing a Trainium2 kernel written in Bass

```python
import numpy as np
import jax
import jax.numpy as jnp

def _softmax(x, axis=-1):
    return jax.nn.softmax(x, axis=axis)
def _gelu(x):
    return jax.nn.gelu(x, approximate=True)
def _silu(x):
    return jax.nn.silu(x)
def _sigmoid(x):
    return jax.nn.sigmoid(x)
def _layernorm(x, axis=-1, eps=1e-5):
    m = jnp.mean(x, axis=axis, keepdims=True)
    v = jnp.var(x, axis=axis, keepdims=True)
    return (x - m) / jnp.sqrt(v + eps)
def _scatter_add(tgt, idx, src, axis=0):
    return tgt.at[idx].add(src)
def _segment_sum(src, seg, n):
    return jax.ops.segment_sum(src, seg, n)

kernel_name = 'mk_conv_preact_d2_conv_nchw192_d9bba0'

def setup_inputs(seed: int = 0):
    np.random.seed(seed)
    _w = jnp.asarray
    def _rec_inputs():
        import jax
        import jax.numpy as jnp
        _gk = jax.random.key(seed)
        x = -0.0002221 + 1 * jax.random.normal(jax.random.fold_in(_gk, 1), (8, 192, 128, 128), jnp.float32)
        return x
    x = _rec_inputs()
    def _L0_conv_setup():
        import jax, jax.numpy as jnp
        import numpy as np
        from jax import lax
        DIM = 192
        HEADS = 4
        EPS = 1e-12

        def _l2norm(t):
            n = jnp.sqrt(jnp.sum(t * t, axis=-1, keepdims=True))
            return t / jnp.maximum(n, EPS)
        key = jax.random.key(seed)
        k1, k2, k3, k4 = jax.random.split(key, 4)
        b, c, h, w = (8, DIM, 128, 128)
        x = jax.random.normal(k1, (b, c, h, w), dtype=jnp.float32)
        w_qkv = jax.random.normal(k2, (3 * c, c), dtype=jnp.float32) * (1.0 / np.sqrt(c))
        w_dw = jax.random.normal(k3, (3 * c, 1, 3, 3), dtype=jnp.float32) * (1.0 / 3.0)
        temperature = jnp.ones((HEADS, 1, 1), dtype=jnp.float32)
        w_proj = jax.random.normal(k4, (c, c), dtype=jnp.float32) * (1.0 / np.sqrt(c))
        return {'x': x, 'w_qkv': w_qkv, 'w_dw': w_dw, 'temperature': temperature, 'w_proj': w_proj}
    _L0_conv_all = _L0_conv_setup()
    _L0_conv_in = {k: v for k, v in _L0_conv_all.items() if k in ('w_qkv', 'w_dw', 'temperature', 'w_proj', )}
    del _L0_conv_all

    def _L1_conv_setup():
        import jax, jax.numpy as jnp
        import numpy as np
        from jax import lax
        B, C, H, W = (8, 192, 224, 224)
        P = 16
        key = jax.random.key(seed)
        k1, k2, k3 = jax.random.split(key, 3)
        X = jax.random.normal(k1, (B, C, H, W), dtype=jnp.float32)
        weights = jax.random.uniform(k2, (C, 1, 1, P), dtype=jnp.float32)
        bias = jax.random.uniform(k3, (C,), dtype=jnp.float32)
        return {'X': X, 'weights': weights, 'bias': bias}
    _L1_conv_all = _L1_conv_setup()
    _L1_conv_in = {k: v for k, v in _L1_conv_all.items() if k in ('weights', 'bias', )}
    del _L1_conv_all

    return {
        "x": x,
        "L0_conv_w_qkv": _L0_conv_in["w_qkv"],
        "L0_conv_w_dw": _L0_conv_in["w_dw"],
        "L0_conv_temperature": _L0_conv_in["temperature"],
        "L0_conv_w_proj": _L0_conv_in["w_proj"],
        "L1_conv_weights": _L1_conv_in["weights"],
        "L1_conv_bias": _L1_conv_in["bias"],
    }

def reference(x, L0_conv_w_qkv, L0_conv_w_dw, L0_conv_temperature, L0_conv_w_proj, L1_conv_weights, L1_conv_bias):
    import jax
    import jax.numpy as jnp
    def _L0_conv_ref(x, w_qkv, w_dw, temperature, w_proj):
        import jax, jax.numpy as jnp
        import numpy as np
        from jax import lax
        DIM = 192
        HEADS = 4
        EPS = 1e-12

        def _l2norm(t):
            n = jnp.sqrt(jnp.sum(t * t, axis=-1, keepdims=True))
            return t / jnp.maximum(n, EPS)
        b, c, h, w = x.shape
        heads = HEADS
        hc = c // heads
        qkv = jnp.einsum('bchw,oc->bohw', x, w_qkv)
        qkv = lax.conv_general_dilated(qkv, w_dw, window_strides=(1, 1), padding='SAME', feature_group_count=3 * c, dimension_numbers=('NCHW', 'OIHW', 'NCHW'))
        q, k, v = jnp.split(qkv, 3, axis=1)
        n = h * w
        q = q.reshape(b, heads, hc, n)
        k = k.reshape(b, heads, hc, n)
        v = v.reshape(b, heads, hc, n)
        q = _l2norm(q)
        k = _l2norm(k)
        attn = jnp.einsum('bhcn,bhdn->bhcd', q, k) * temperature[None]
        attn = jax.nn.softmax(attn, axis=-1)
        out = jnp.einsum('bhcd,bhdn->bhcn', attn, v)
        out = out.reshape(b, c, h, w)
        out = jnp.einsum('bchw,oc->bohw', out, w_proj)
        return out

    def _L1_conv_ref(X, weights, bias):
        import jax, jax.numpy as jnp
        import numpy as np
        from jax import lax
        B, C, H, W = (8, 192, 224, 224)
        P = 16
        X_cat = jnp.concatenate([X, X[:, :, :, :-1]], axis=-1)
        target_width = X_cat.shape[2]
        idx = jnp.arange(target_width) * P // target_width
        kernel = weights[:, :, :, idx]
        out = lax.conv_general_dilated(X_cat, kernel, window_strides=(1, 1), padding='VALID', feature_group_count=C, dimension_numbers=('NCHW', 'OIHW', 'NCHW'))
        return out + bias[None, :, None, None]

    def _gn(v, G=32, eps=1e-5):
        B_, C_, H_, W_ = v.shape
        g = v.reshape(B_, G, C_ // G, H_, W_)
        m = jnp.mean(g, axis=(2, 3, 4), keepdims=True)
        s = jnp.var(g, axis=(2, 3, 4), keepdims=True)
        return ((g - m) / jnp.sqrt(s + eps)).reshape(v.shape)

    def _ln_c(v, eps=1e-6):
        m = jnp.mean(v, axis=1, keepdims=True)
        s = jnp.var(v, axis=1, keepdims=True)
        return (v - m) / jnp.sqrt(s + eps)

    def _ln_t(v, eps=1e-5):
        m = jnp.mean(v, axis=-1, keepdims=True)
        s = jnp.var(v, axis=-1, keepdims=True)
        return (v - m) / jnp.sqrt(s + eps)

    def _to_tokens(v):
        B_, C_, H_, W_ = v.shape
        return v.reshape(B_, C_, H_ * W_).transpose(0, 2, 1)
    def _from_tokens(t, like):
        B_, C_, H_, W_ = like.shape
        return t.transpose(0, 2, 1).reshape(B_, C_, H_, W_)

    x = x + _L0_conv_ref(_gn(x), L0_conv_w_qkv, L0_conv_w_dw, L0_conv_temperature, L0_conv_w_proj)
    x = x + _L1_conv_ref(_gn(x), L1_conv_weights, L1_conv_bias)
    return x


_drawn_inputs = setup_inputs


def setup_inputs(seed=0):
    import zlib

    import numpy as np

    out = dict(_drawn_inputs(seed))
    spreads = {'L0_conv_temperature': (1.0, 0.2)}
    factors = {}
    for name, (base, spread) in spreads.items():
        noise = np.random.default_rng([zlib.crc32(name.encode()), seed]).standard_normal(out[name].shape)
        drawn = base * np.exp(spread * noise) if base else spread * noise
        out[name] = jnp.asarray(drawn.astype(out[name].dtype))
    for name, factor in factors.items():
        out[name] = (out[name] * factor).astype(out[name].dtype)
    return out
```

```python
import concourse.bass as bass
from concourse import mybir
from contextlib import ExitStack

B, C, H, W = 8, 192, 128, 128
HEADS, HC = 4, 48
GROUPS, GC = 32, 6
TAPS = 9
PIECES, PIECE = 16, 8
EPS = 1e-5
NORM_EPS = 1e-12

P = 128
CA = 128
CB = C - CA
PITCH = W + 1
IMAGE = (H + 2) * PITCH + 1
ROWS = 8
CHUNKS = H // ROWS
STEP = ROWS * PITCH
WINDOW = (ROWS + 2) * PITCH + 1
LOAD_ROWS = 4
LOADS = H // LOAD_ROWS
NLOAD = LOAD_ROWS * W
QK = 2 * C
HQK = 2 * HC
PAIRS = ROWS // 2
UP = 64.0
N_GROUP = GC * H * W
CG = 24
CGROUPS = C // CG
QUAD = 4
QUADS = CG // QUAD


def conv_kernel(nc, x, w_qk, w_v, w_dw_qk, w_dw_v, w_proj_t, temperature, wide_w, wide_t, bias,
                group_a, group_b, ident_in, res_eye_in, out):
    f32, f16 = mybir.dt.float32, mybir.dt.float16
    ALU = mybir.AluOpType
    ACT = mybir.ActivationFunctionType
    AX = mybir.AxisListType

    ctx = ExitStack()
    with ctx:
        def sb(name, shape, dt=f32):
            return stack[-1].enter_context(nc.sbuf_tensor(name, shape, dt))

        def sem(name):
            return ctx.enter_context(nc.semaphore(name))

        stack = [ctx]
        z_dram = nc.dram_tensor("z_scratch", [B, P, CGROUPS, H, 2, CG], f16).ap()
        tab_dram = nc.dram_tensor("wide_table", [C, 2, 2 * W], f16).ap()

        t_mean = sb("t_mean", [P, B, GROUPS])
        t_sd = sb("t_sd", [P, B, GROUPS])
        t_s1 = sb("t_s1", [P, B, GROUPS])
        t_s1m = sb("t_s1m", [P, B, GROUPS])
        ident = sb("ident", [P, P])
        ident16 = sb("ident16", [P, P], f16)
        ones = sb("ones", [P, P])

        psum = [ctx.enter_context(nc.psum_tensor(f"bank{i}", [P, 512], f32)) for i in range(8)]
        acc, gram, misc = psum[0:4], psum[4:6], psum[6:8]

        layer0 = ExitStack()
        layer0_block = ExitStack()
        stack.append(layer0)
        xa_hi = sb("xa_hi", [P, IMAGE], f16)
        xa_lo = sb("xa_lo", [P, IMAGE], f16)
        xb = sb("xb", [P, IMAGE], f16)
        e_qk = sb("e_qk", [P, 2, 2, TAPS, QK], f16)
        e_v = sb("e_v", [P, 2, 2, TAPS, C], f16)
        qk = sb("qk", [P, 4, HEADS, 2, HQK], f16)
        stage = sb("stage", [P, 2, 2, NLOAD])
        stage_hi = sb("stage_hi", [P, NLOAD], f16)
        zf = sb("zf", [P, 2, 2 * C])
        z_out = sb("z_out", [P, CGROUPS, ROWS, 2, CG], f16)
        sum_z = sb("sum_z", [P, 2 * C])
        sum_q = sb("sum_q", [P, 2 * C])
        sq = sb("sq", [P, 2 * C])
        grp_a = sb("grp_a", [P, 2 * P])
        grp_b = sb("grp_b", [P, 2 * P])
        res_eye = sb("res_eye", [P, 2, C])
        wv = sb("wv", [HC, HEADS, 2, P])
        wdv = sb("wdv", [HC, HEADS, TAPS])
        wpt = sb("wpt", [HC, HEADS, C])
        temp = sb("temp", [HC, HEADS])
        mt = sb("mt", [HC, HEADS, C])
        dm = sb("dm", [HC, 2, HEADS, C])
        stats = sb("stats", [P, 2, LOADS, 6])
        mv = sb("mv", [P, 2, 2])
        col = sb("col", [P, 2, 2])
        colb = sb("colb", [P, 2, 2, P])
        st_m = sb("st_m", [P, GROUPS + 2])
        st_v = sb("st_v", [P, GROUPS + 2])
        st_t = sb("st_t", [P, GROUPS + 2])
        nbias = sb("nbias", [P, 2])
        r0up = sb("r0up", [P, C])
        zeros = sb("zeros", [P, QK], f16)

        gs = sb("gs", [HQK, HEADS, 2 * HQK])
        gg = sb("gg", [HQK, HEADS, HQK])
        gt = sb("gt", [HQK, HEADS, HQK])
        kn = sb("kn", [HC, HEADS, HC])
        qn = sb("qn", [HC, HEADS])
        attn = sb("attn", [HC, HEADS, HC])
        small = sb("small", [HC, HEADS])
        esum = sb("esum", [P, 2, C])

        carried = sem("carried")
        const_loaded = sem("const_loaded")
        loaded = [sem("loaded0"), sem("loaded1")]
        stats_used = sem("stats_used")
        taps_loaded = [sem("taps_loaded0"), sem("taps_loaded1")]
        taps_folded = sem("taps_folded")
        pads_zero = sem("pads_zero")
        consts_made = sem("consts_made")
        table_made = sem("table_made")
        table_stored = sem("table_stored")
        affine = sem("affine")
        hi_made = sem("hi_made")
        normed = sem("normed")
        acc_full = sem("acc_full")
        qk_hi = sem("qk_hi")
        qk_split = sem("qk_split")
        gram_rows = sem("gram_rows")
        z_copied = sem("z_copied")
        z_split = sem("z_split")
        z_summed = sem("z_summed")
        z_stored = sem("z_stored")
        sums_zero = sem("sums_zero")
        pool_step = sem("pool_step")
        zsum_ps = sem("zsum_ps")
        zsum_read = sem("zsum_read")
        st_read = sem("st_read")
        step_v = sem("step_v")
        st_col = sem("st_col")
        st_ps = sem("st_ps")
        var_made = sem("var_made")
        sd_made = sem("sd_made")
        gram_copied = sem("gram_copied")
        gram_closed = sem("gram_closed")
        gram_t = sem("gram_t")
        diag_made = sem("diag_made")
        colsum = sem("colsum")
        norms_ready = sem("norms_ready")
        norms_rooted = sem("norms_rooted")
        logits = sem("logits")
        exped = sem("exped")
        attn_made = sem("attn_made")
        mt_ps = sem("mt_ps")
        dm_made = sem("dm_made")
        e_ps = sem("e_ps")
        e_sum = sem("e_sum")
        e_hi = sem("e_hi")
        e_lo = sem("e_lo")

        table = z_out[0:HQK, :, :, :, :].rearrange("p g r s c -> p (g r s c)")[:, 0:4 * 2 * W]\
            .rearrange("p (a s n) -> p a s n", a=2, s=2)

        def settled(engine):
            engine.sem_inc(carried, 1)

        def block_of(i):
            return (xa_hi, xa_lo, xb)[i]

        def body_rows(tensor, chunk, first):
            win = tensor[:, bass.ds(chunk * STEP, WINDOW)]
            v = win[:, 0:(ROWS + 2) * PITCH].rearrange("p (r c) -> p r c", c=PITCH)
            return v[:, 1 + first:1 + first + LOAD_ROWS, 1:1 + W]

        def rows(ap):
            return ap.rearrange("p (r c) -> p r c", c=W)

        PRODUCTS = [(0, 0, 0), (0, 1, 0), (1, 0, 0), (2, 0, 1), (2, 1, 1)]
        N_CONST = 15

        block = layer0_block.enter_context(nc.Block())

        @block.sync
        def _(sp):
            for dst, src in (
                (grp_a[:, :], group_a), (grp_b[:, :], group_b), (ident[:, :], ident_in),
                (res_eye[:, :, :], res_eye_in),
                (wv[:, :, 0, :], w_v[:, 0:CA].rearrange("(h p) i -> p h i", p=HC)),
                (wv[:, :, 1, 0:CB], w_v[:, CA:C].rearrange("(h p) i -> p h i", p=HC)),
                (wv[:, :, 1, CB:P], w_v[:, CA:C].rearrange("(h p) i -> p h i", p=HC)),
                (wdv[:, :, :], w_dw_v.rearrange("(h p) t -> p h t", p=HC)),
                (wpt[:, :, :], w_proj_t.rearrange("(h p) o -> p h o", p=HC)),
                (temp[:, :], temperature.rearrange("(a h) -> a h", a=1).to_broadcast([HC, HEADS])),
                (stage[:, 0, 0, 0:QK], w_qk[0:CA, :]),
                (stage[0:CB, 0, 1, 0:QK], w_qk[CA:C, :]),
                (stage[CB:P, 0, 1, 0:QK], w_qk[CA:C, :]),
                (gs[:, 0, 0:PIECES], wide_w[0:HQK, :]),
            ):
                sp.dma_start(dst, src).then_inc(const_loaded, 16)
            sp.dma_start(gs[:, 1, 0:PIECES], wide_w[HQK:C, :]).then_inc(const_loaded, 16)
            for t in range(TAPS):
                if t >= 2:
                    sp.wait_ge(taps_folded, t - 1)
                sp.dma_start(stage[:, 1, t % 2, 0:QK], w_dw_qk[t:t + 1, :].to_broadcast([P, QK])).then_inc(taps_loaded[t % 2], 16)
            sp.wait_ge(table_made, 2)
            for part in range(2):
                sp.dma_start(tab_dram[part * HQK:(part + 1) * HQK, :, :], table[:, part, :, :]).then_inc(table_stored, 16)
            sp.wait_ge(taps_folded, TAPS)

            def load(b, j, slot):
                rows_of = bass.ds(j * ROWS + slot * LOAD_ROWS, LOAD_ROWS)
                for dst, c0, c1 in ((stage[:, slot, 0, :], 0, CA), (stage[0:CB, slot, 1, :], CA, C),
                                    (stage[CB:P, slot, 1, :], CA, C)):
                    sp.dma_start(dst, x[bass.ds(b, 1), c0:c1, rows_of, :].rearrange("b c h w -> c (b h w)"))\
                        .then_inc(loaded[slot], 16)

            def load_for_stats(b):
                sp.wait_ge(normed, 2 + b * (LOADS + 1))
                settled(sp)
                with sp.Fori(0, CHUNKS) as j:
                    for slot in range(2):
                        sp.wait_ge(stats_used, b * LOADS + j * 2 + slot + 1)
                        load(b, j, slot)
                sp.wait_ge(stats_used, 2 + b * LOADS + LOADS)
                settled(sp)

            def load_to_normalise(b, j):
                for slot in range(2):
                    sp.wait_ge(normed, b * (LOADS + 1) + j * 2 + slot + 1)
                    load(b, j, slot)

            def store_z(b, j):
                sp.wait_ge(z_split, 1 + b * (H // 2) + j * PAIRS + PAIRS)
                sp.dma_start(z_dram[bass.ds(b, 1), :, :, bass.ds(j * ROWS, ROWS), :, :].rearrange("b p g r s c -> p (b g) (r s c)"),
                             z_out[:, :, :, :, :].rearrange("p g r s c -> p g (r s c)")).then_inc(z_stored, 16)

            load_for_stats(0)
            with sp.Fori(0, CHUNKS) as j:
                load_to_normalise(0, j)
            with sp.Fori(0, B - 1) as b:
                load_for_stats(b + 1)
                with sp.Fori(0, CHUNKS) as j:
                    load_to_normalise(b + 1, j)
                    store_z(b, j)
            with sp.Fori(0, CHUNKS) as j:
                store_z(B - 1, j)
            sp.wait_ge(z_stored, 16 + 16 * B * CHUNKS)
            sp.wait_ge(table_stored, 32)

        @block.gpsimd
        def _(pool):
            for t in (xa_hi, xa_lo, xb):
                nc.gpsimd.memset(t[:, :], 0.0).then_inc(pads_zero, 1)
            nc.gpsimd.memset(zeros[:, :], 0.0).then_inc(pads_zero, 1)
            nc.gpsimd.memset(ones[:, :], 1.0).then_inc(pads_zero, 1)

            with pool.Fori(0, B) as b:
                pool.wait_ge(zsum_ps, 1 + b)
                settled(pool)
                nc.gpsimd.memset(sum_z[:, :], 0.0).then_inc(sums_zero, 1)
                nc.gpsimd.memset(sum_q[:, :], 0.0).then_inc(sums_zero, 1)
                pool.wait_ge(sums_zero, b * 2 + 2)
                settled(pool)
                with pool.Fori(0, H // 4) as j:
                    for s in range(2):
                        n = b * (H // 2) + j * 2 + s
                        pool.wait_ge(z_copied, 4 + n + 1)
                        pool.wait_ge(z_summed, 1 + n)
                        nc.gpsimd.tensor_tensor(sq[:, :], zf[:, s, :], zf[:, s, :], ALU.mult).then_inc(pool_step, 1)
                        nc.gpsimd.tensor_tensor(sum_z[:, :], sum_z[:, :], zf[:, s, :], ALU.add).then_inc(pool_step, 1)
                        pool.wait_ge(pool_step, n * 2 + 2)
                        nc.gpsimd.tensor_tensor(sum_q[:, :], sum_q[:, :], sq[:, :], ALU.add).then_inc(z_summed, 1)

        @block.scalar
        def _(act):
            act.wait_ge(const_loaded, 16 * N_CONST)
            nc.scalar.activation(ident16[:, :], ident[:, :], ACT.Copy).then_inc(consts_made, 1)

            def normalise_hi(b, j, slot):
                n = b * LOADS + j * 2 + slot
                act.wait_ge(affine, n * 2 + 2)
                nc.scalar.activation(body_rows(xa_hi, j, slot * LOAD_ROWS), rows(stage[:, slot, 0, :]), ACT.Copy)\
                    .then_inc(hi_made, 1)
                nc.scalar.activation(body_rows(xb, j, slot * LOAD_ROWS)[0:CB], rows(stage[0:CB, slot, 1, :]), ACT.Copy)\
                    .then_inc(hi_made, 1)
                act.wait_ge(normed, 2 + b * (LOADS + 1) + j * 2 + slot)
                nc.scalar.activation(stage_hi[CB:P, :], stage[CB:P, slot, 1, :], ACT.Copy).then_inc(hi_made, 1)

            def root(n, width):
                act.wait_ge(var_made, n)
                nc.scalar.activation(st_t[:, 0:width], st_v[:, 0:width], ACT.Sqrt).then_inc(sd_made, 1)

            def qk_rows(b, j):
                for r in range(ROWS):
                    row = b * H + j * ROWS + r
                    act.wait_ge(acc_full, b * (H + H // 2) + j * ROWS + r + 1)
                    act.wait_ge(gram_rows, row + 1)
                    nc.scalar.activation(qk[:, r % 4, :, 0, :], acc[r % 4][:, 0:QK].rearrange("p (h c) -> p h c", h=HEADS),
                                         ACT.Copy).then_inc(qk_hi, 1)

            def z_pair(b, j, r):
                pair = b * (H // 2) + j * PAIRS + r
                act.wait_ge(acc_full, b * (H + H // 2) + H + j * PAIRS + r + 1)
                if r == 0:
                    act.wait_ge(z_stored, 16 + (b * CHUNKS + j) * 16)
                act.wait_ge(z_split, 1 + pair)
                act.wait_ge(z_summed, 1 + pair)
                for i in range(2):
                    nc.scalar.activation(z_out[:, :, 2 * r + i, 0, :],
                                         acc[r % 4][:, i * C:(i + 1) * C].rearrange("p (g c) -> p g c", c=CG),
                                         ACT.Copy, scale=1.0 / UP)
                nc.scalar.activation(zf[:, r % 2, :], acc[r % 4][:, 0:2 * C], ACT.Copy, scale=1.0 / UP)\
                    .then_inc(z_copied, 1)

            def attention(b):
                act.wait_ge(norms_ready, b * 2 + 2)
                nc.scalar.activation(kn[:, :, :], gt[0:HC, :, HC:HQK], ACT.Sqrt).then_inc(norms_rooted, 1)
                nc.scalar.activation(qn[:, :], small[:, :], ACT.Sqrt).then_inc(norms_rooted, 1)
                act.wait_ge(logits, b + 1)
                nc.scalar.activation(gt[0:HC, :, 0:HC], attn[:, :, :], ACT.Exp).then_inc(exped, 1)
                for t in range(TAPS):
                    act.wait_ge(e_sum, b * TAPS + t + 1)
                    nc.scalar.activation(e_v[:, 0, :, t, :], esum[:, :, :], ACT.Copy).then_inc(e_hi, 1)

            def image(b, ahead):
                with act.Fori(0, CHUNKS) as j:
                    qk_rows(b, j)
                attention(b)
                if ahead:
                    root(b * 2 + 2, GROUPS + 2)
                for r in range(PAIRS):
                    z_pair(b, 0, r)
                with act.Fori(1, CHUNKS) as j:
                    for r in range(PAIRS):
                        z_pair(b, j, r)
                        if ahead and r >= 1 and r < 3:
                            normalise_hi(b + 1, j - 1, r - 1)
                if ahead:
                    for slot in range(2):
                        normalise_hi(b + 1, CHUNKS - 1, slot)
                root(b * 2 + 3 if ahead else b * 2 + 2, GROUPS)

            act.wait_ge(pads_zero, 5)
            root(1, GROUPS + 2)
            with act.Fori(0, CHUNKS) as j:
                for slot in range(2):
                    normalise_hi(0, j, slot)
            act.wait_ge(table_stored, 32)
            with act.Fori(0, B - 1) as b:
                image(b, True)
            image(B - 1, False)

        @block.tensor
        def _(pe):
            def row_products(bank, base, weights, n, win, r):
                k = 0
                for t in range(TAPS):
                    at = (r + t // 3) * PITCH + t % 3
                    for blk, half, wblk in PRODUCTS:
                        last = nc.tensor.matmul(bank[:, base:base + n], win[blk][:, at:at + W],
                                                weights[:, half, wblk, t, :], start=k == 0,
                                                stop=k == TAPS * len(PRODUCTS) - 1, skip_group_check=True)
                        k += 1
                return last

            def windows(j):
                return [block_of(i)[:, bass.ds(j * STEP, WINDOW)] for i in range(3)]

            def gram_row(b, j, r):
                pe.wait_ge(qk_split, 4 + b * H + j * ROWS + r + 1)
                for h in range(HEADS):
                    at = (h % 2) * 2 * HQK
                    last = nc.tensor.matmul(gram[h // 2][0:HQK, at:at + 2 * HQK], qk[:, r % 4, h, 0, :],
                                            qk[:, r % 4, h, :, :].rearrange("p s c -> p (s c)"),
                                            start=False, stop=False, skip_group_check=True)
                last.then_inc(gram_rows, 1)

            def stats_sums(n):
                pe.wait_ge(st_col, n)
                for s in range(2):
                    for i, g in enumerate((grp_a, grp_b)):
                        nc.tensor.matmul(misc[0][:, s * C:(s + 1) * C], colb[:, i, s, :], g[:, 0:C],
                                         start=i == 0, stop=i == 1, skip_group_check=True)
                for m in range(2):
                    for i, g in enumerate((grp_a, grp_b)):
                        last = nc.tensor.matmul(misc[1][:, 2 * m:2 * m + 2], g[:, m * P:(m + 1) * P], col[:, i, :],
                                                start=i == 0, stop=i == 1, skip_group_check=True)
                last.then_inc(st_ps, 1)

            def image(b, ahead):
                pe.wait_ge(z_copied, 4 + b * (H // 2))
                pe.wait_ge(gram_copied, 2 + b * 2)
                for g in gram:
                    nc.tensor.matmul(g[0:HQK, 0:QK], zeros[:, 0:HQK], zeros[:, :], start=True, stop=False,
                                     skip_group_check=True)
                with pe.Fori(0, CHUNKS) as j:
                    win = windows(j)
                    pe.wait_ge(normed, 2 + b * (LOADS + 1) + j * 2 + 3)
                    for r in range(ROWS):
                        pe.wait_ge(qk_split, b * H + j * ROWS + r + 1)
                        row_products(acc[r % 4], 0, e_qk, QK, win, r).then_inc(acc_full, 1)
                        if r:
                            gram_row(b, j, r - 1)
                    gram_row(b, j, ROWS - 1)
                for g in gram:
                    last = nc.tensor.matmul(g[0:HQK, 0:QK], zeros[:, 0:HQK], zeros[:, :], start=False, stop=True,
                                            skip_group_check=True)
                last.then_inc(gram_closed, 1)
                pe.wait_ge(gram_copied, 2 + b * 2 + 2)
                pe.wait_ge(zsum_read, 1 + b)
                for h in range(HEADS):
                    last = nc.tensor.transpose(misc[0][0:HQK, h * HQK:(h + 1) * HQK], gs[:, h, HQK:2 * HQK],
                                               ident[0:HQK, 0:HQK])
                last.then_inc(gram_t, 1)
                pe.wait_ge(diag_made, b + 1)
                nc.tensor.matmul(misc[1][0:HQK, 0:QK], ones[0:HQK, 0:HQK], gt[:, :, :].rearrange("p h c -> p (h c)"),
                                 start=True, stop=True).then_inc(colsum, 1)
                pe.wait_ge(attn_made, b + 1)
                settled(pe)
                for h in range(HEADS):
                    last = nc.tensor.matmul(misc[h // 2][0:HC, (h % 2) * C:(h % 2 + 1) * C], attn[:, h, :], wpt[:, h, :],
                                            start=True, stop=True, skip_group_check=True)
                last.then_inc(mt_ps, 1)
                for t in range(TAPS):
                    pe.wait_ge(dm_made, b * TAPS + t + 1)
                    if t >= 2:
                        pe.wait_ge(e_sum, b * TAPS + t - 1)
                    for i in range(2):
                        for h in range(HEADS):
                            last = nc.tensor.matmul(misc[t % 2][:, i * C:(i + 1) * C], wv[:, h, i, :], dm[:, t % 2, h, :],
                                                    start=h == 0, stop=h == HEADS - 1, skip_group_check=True)
                    last.then_inc(e_ps, 1)
                if ahead:
                    pe.wait_ge(e_sum, b * TAPS + TAPS)
                    stats_sums(b + 2)
                pe.wait_ge(e_lo, 1 + b * TAPS + TAPS)
                settled(pe)
                with pe.Fori(0, CHUNKS) as j:
                    win = windows(j)
                    for r in range(PAIRS):
                        pe.wait_ge(z_copied, b * (H // 2) + j * PAIRS + r + 1)
                        row_products(acc[r], 0, e_v, C, win, 2 * r)
                        row_products(acc[r], C, e_v, C, win, 2 * r + 1).then_inc(acc_full, 1)
                pe.wait_ge(z_summed, 1 + b * (H // 2) + H // 2)
                if ahead:
                    pe.wait_ge(st_read, b + 2)
                nc.tensor.matmul(misc[0][:, 0:2 * C], ones[:, :], sum_z[:, :], start=True, stop=True)
                nc.tensor.matmul(misc[1][:, 0:2 * C], ones[:, :], sum_q[:, :], start=True, stop=True).then_inc(zsum_ps, 1)

            pe.wait_ge(const_loaded, 16 * N_CONST)
            pe.wait_ge(pads_zero, 5)
            pe.wait_ge(taps_folded, TAPS)
            stats_sums(1)
            with pe.Fori(0, B - 1) as b:
                image(b, True)
            image(B - 1, False)

        @block.vector
        def _(dve):
            chain = [0, 0]
            LINKS = 33

            def link(ins):
                chain[1] += 1
                ins.then_inc(step_v, 1)
                dve.wait_ge(step_v, chain[0] + chain[1])

            dve.wait_ge(const_loaded, 16 * N_CONST)
            for free, n in ((qk_split, 4), (z_copied, 4), (gram_rows, 4), (stats_used, 2), (normed, 2), (gram_copied, 2),
                            (zsum_ps, 1), (zsum_read, 1), (z_summed, 1), (z_split, 1), (e_lo, 1), (z_stored, 16)):
                dve.sem_inc(free, n)
            for t in range(TAPS):
                dve.wait_ge(taps_loaded[t % 2], 16 * (t // 2 + 1))
                for i in range(2):
                    link(nc.vector.scalar_tensor_tensor(zf[:, i, :], stage[:, 0, i, 0:QK], UP, stage[:, 1, t % 2, 0:QK],
                                                        ALU.mult, ALU.mult))
                    link(nc.vector.tensor_copy(e_qk[:, 0, i, t, :], zf[:, i, :]))
                    link(nc.vector.tensor_tensor(e_qk[:, 1, i, t, :], zf[:, i, :], e_qk[:, 0, i, t, :], ALU.subtract))
                dve.sem_inc(taps_folded, 1)
            for part in range(2):
                src = gs[:, part, 0:PIECES].rearrange("p (n c) -> p n c", c=1).to_broadcast([HQK, PIECES, PIECE])
                for a in range(2):
                    hi, lo = [table[:, part, s, a * W:(a + 1) * W].rearrange("p (n c) -> p n c", c=PIECE) for s in range(2)]
                    link(nc.vector.tensor_copy(hi, src))
                    link(nc.vector.tensor_tensor(lo, src, hi, ALU.subtract))
                dve.sem_inc(table_made, 1)

            def load_wait(b, half, j, slot):
                dve.wait_ge(loaded[slot], (b * (2 * CHUNKS) + half * CHUNKS + j + 1) * 48)

            def stats_load(b, j, slot):
                load_wait(b, 0, j, slot)
                for i in range(2):
                    last = nc.vector.bn_stats(stats[:, i, bass.ds(j * 2 + slot, 1), :].rearrange("p a s -> p (a s)"),
                                              stage[:, slot, i, :])
                last.then_inc(stats_used, 1)

            def stats_final(b, turn):
                dve.wait_ge(stats_used, 2 + b * LOADS + LOADS)
                settled(dve)
                nc.vector.bn_aggr(mv[:, 0, :], stats[:, 0, :, :].rearrange("p n s -> p (n s)"))
                link(nc.vector.bn_aggr(mv[:, 1, :], stats[:, 1, :, :].rearrange("p n s -> p (n s)")))
                nc.vector.tensor_copy(col[:, :, 0], mv[:, :, 0])
                link(nc.vector.tensor_tensor(col[:, :, 1], mv[:, :, 0], mv[:, :, 0], ALU.mult))
                link(nc.vector.tensor_tensor(col[:, :, 1], col[:, :, 1], mv[:, :, 1], ALU.add))
                nc.vector.tensor_copy(colb[:, :, :, :], col[:, :, :].rearrange("p i (s a) -> p i s a", a=1)
                                      .to_broadcast([P, 2, 2, P])).then_inc(st_col, 1)
                dve.wait_ge(st_ps, b + 1)
                sums = misc[0][:, 0:2 * C].rearrange("p (s g c) -> p s g c", s=2, c=GC)
                nc.vector.tensor_copy(st_m[:, 0:GROUPS], sums[:, 0, :, 0])
                nc.vector.tensor_copy(st_v[:, 0:GROUPS], sums[:, 1, :, 0])
                nc.vector.tensor_copy(st_m[:, GROUPS:], misc[1][:, 0:4:2])
                nc.vector.tensor_copy(st_v[:, GROUPS:], misc[1][:, 1:4:2]).then_inc(st_read, 1)
                dve.wait_ge(st_read, b + 1)
                link(nc.vector.tensor_tensor(st_t[:, :], st_m[:, :], st_m[:, :], ALU.mult))
                link(nc.vector.tensor_tensor(st_v[:, :], st_v[:, :], st_t[:, :], ALU.subtract))
                nc.vector.tensor_scalar(st_v[:, :], st_v[:, :], 0.0, EPS, ALU.max, ALU.add).then_inc(var_made, 1)
                dve.wait_ge(sd_made, turn)
                nc.vector.tensor_copy(t_sd[:, bass.ds(b, 1), :].rearrange("p a g -> p (a g)"), st_t[:, 0:GROUPS])
                nc.vector.tensor_copy(t_mean[:, bass.ds(b, 1), :].rearrange("p a g -> p (a g)"), st_m[:, 0:GROUPS])
                link(nc.vector.reciprocal(st_v[:, :], st_t[:, :]))
                nc.vector.scalar_tensor_tensor(nbias[:, :], st_m[:, GROUPS:], -1.0, st_v[:, GROUPS:], ALU.mult, ALU.mult)
                link(nc.vector.tensor_scalar(r0up[:, :].rearrange("p (g c) -> p g c", c=GC),
                                             st_v[:, 0:GROUPS].rearrange("p (g a) -> p g a", a=1).to_broadcast([P, GROUPS, GC]),
                                             UP, None, ALU.mult))

            def normalise_scale(b, j, slot):
                load_wait(b, 1, j, slot)
                for i in range(2):
                    nc.vector.tensor_scalar(stage[:, slot, i, :], stage[:, slot, i, :], st_v[:, GROUPS + i:GROUPS + i + 1],
                                            nbias[:, i:i + 1], ALU.mult, ALU.add).then_inc(affine, 1)

            def normalise_lo(b, j, slot):
                n = b * LOADS + j * 2 + slot
                dve.wait_ge(hi_made, n * 3 + 3)
                first = slot * LOAD_ROWS
                nc.vector.tensor_tensor(body_rows(xa_lo, j, first), rows(stage[:, slot, 0, :]), body_rows(xa_hi, j, first),
                                        ALU.subtract)
                nc.vector.tensor_tensor(body_rows(xb, j, first)[CB:P], rows(stage[CB:P, slot, 1, :]), rows(stage_hi[CB:P, :]),
                                        ALU.subtract).then_inc(normed, 1)

            def end_of_image(b):
                dve.wait_ge(normed, 2 + b * (LOADS + 1) + LOADS)
                dve.sem_inc(normed, 1)

            def attention(b):
                dve.wait_ge(gram_closed, b + 1)
                for g in range(2):
                    nc.vector.tensor_copy(gs[:, 2 * g:2 * g + 2, :], gram[g][0:HQK, 0:QK].rearrange("p (h c) -> p h c", h=2))\
                        .then_inc(gram_copied, 1)
                dve.wait_ge(gram_t, b + 1)
                dve.wait_ge(gram_copied, 2 + b * 2 + 2)
                link(nc.vector.tensor_tensor(gg[:, :, :], gs[:, :, 0:HQK], gs[:, :, HQK:2 * HQK], ALU.add))
                link(nc.vector.tensor_tensor(gg[:, :, :], misc[0][0:HQK, 0:QK].rearrange("p (h c) -> p h c", h=HEADS),
                                             gg[:, :, :], ALU.add))
                eye = ident[0:HQK, 0:HQK].rearrange("p (a c) -> p a c", a=1).to_broadcast([HQK, HEADS, HQK])
                nc.vector.tensor_tensor(gt[:, :, :], gg[:, :, :], eye, ALU.mult).then_inc(diag_made, 1)
                dve.wait_ge(diag_made, b + 1)
                link(nc.vector.tensor_reduce(small[:, :], gt[0:HC, :, 0:HC], AX.X, ALU.add))
                nc.vector.tensor_scalar(small[:, :], small[:, :], 0.0, None, ALU.max).then_inc(norms_ready, 1)
                dve.wait_ge(colsum, b + 1)
                nc.vector.tensor_scalar(gt[0:HC, :, HC:HQK],
                                        misc[1][0:HC, 0:QK].rearrange("p (h c) -> p h c", h=HEADS)[:, :, HC:HQK],
                                        0.0, None, ALU.max).then_inc(norms_ready, 1)
                dve.wait_ge(norms_rooted, b * 2 + 2)
                link(nc.vector.tensor_scalar(kn[:, :, :], kn[:, :, :], NORM_EPS * UP, None, ALU.max))
                link(nc.vector.tensor_scalar(qn[:, :], qn[:, :], NORM_EPS * UP, None, ALU.max))
                link(nc.vector.reciprocal(kn[:, :, :], kn[:, :, :]))
                link(nc.vector.reciprocal(qn[:, :], qn[:, :]))
                link(nc.vector.tensor_tensor(qn[:, :], qn[:, :], temp[:, :], ALU.mult))
                link(nc.vector.tensor_tensor(attn[:, :, :], gg[0:HC, :, HC:HQK], kn[:, :, :], ALU.mult))

                def over(t):
                    return t[:, :].rearrange("p (h a) -> p h a", a=1).to_broadcast([HC, HEADS, HC])

                link(nc.vector.tensor_tensor(attn[:, :, :], attn[:, :, :], over(qn), ALU.mult))
                link(nc.vector.tensor_reduce(small[:, :], attn[:, :, :], AX.X, ALU.max))
                nc.vector.tensor_tensor(attn[:, :, :], attn[:, :, :], over(small), ALU.subtract).then_inc(logits, 1)
                dve.wait_ge(exped, b + 1)
                link(nc.vector.tensor_reduce(small[:, :], gt[0:HC, :, 0:HC], AX.X, ALU.add))
                link(nc.vector.reciprocal(small[:, :], small[:, :]))
                nc.vector.tensor_tensor(attn[:, :, :], gt[0:HC, :, 0:HC], over(small), ALU.mult).then_inc(attn_made, 1)
                dve.wait_ge(mt_ps, b + 1)
                for g in range(2):
                    link(nc.vector.tensor_tensor(mt[:, 2 * g:2 * g + 2, :],
                                                 misc[g][0:HC, 0:2 * C].rearrange("p (h c) -> p h c", h=2),
                                                 r0up[0:HC, :].rearrange("p (a c) -> p a c", a=1).to_broadcast([HC, 2, C]),
                                                 ALU.mult))

                def fold(t):
                    n = b * TAPS + t
                    if t >= 2:
                        dve.wait_ge(e_ps, n - 1)
                    nc.vector.tensor_tensor(dm[:, t % 2, :, :], mt[:, :, :],
                                            wdv[:, :, t:t + 1].to_broadcast([HC, HEADS, C]), ALU.mult).then_inc(dm_made, 1)

                fold(0)
                for t in range(TAPS):
                    n = b * TAPS + t
                    if t + 1 < TAPS:
                        fold(t + 1)
                    dve.wait_ge(e_ps, n + 1)
                    dve.wait_ge(e_lo, 1 + n)
                    src = misc[t % 2][:, 0:2 * C].rearrange("p (i c) -> p i c", i=2)
                    if t == TAPS // 2:
                        nc.vector.tensor_tensor(esum[:, :, :], src, res_eye[:, :, :], ALU.add).then_inc(e_sum, 1)
                    else:
                        nc.vector.tensor_copy(esum[:, :, :], src).then_inc(e_sum, 1)
                    dve.wait_ge(e_hi, n + 1)
                    nc.vector.tensor_tensor(e_v[:, 1, :, t, :], esum[:, :, :], e_v[:, 0, :, t, :], ALU.subtract)\
                        .then_inc(e_lo, 1)

            def z_final(b, ahead):
                dve.wait_ge(zsum_ps, 1 + b + 1)
                dve.wait_ge(sd_made, b * 2 + 2 if ahead else b * 2 + 1)
                for i, t in enumerate((st_m, st_v)):
                    link(nc.vector.tensor_reduce(t[:, 0:GROUPS],
                                                 misc[i][:, 0:2 * C].rearrange("p (r g c) -> p g r c", r=2, c=GC),
                                                 AX.XY, ALU.add))
                dve.sem_inc(zsum_read, 1)
                link(nc.vector.tensor_scalar(st_v[:, 0:GROUPS], st_v[:, 0:GROUPS], 1.0 / N_GROUP, None, ALU.mult))
                link(nc.vector.tensor_scalar(st_m[:, 0:GROUPS], st_m[:, 0:GROUPS], 1.0 / N_GROUP, None, ALU.mult))
                sd0 = t_sd[:, bass.ds(b, 1), :].rearrange("p a g -> p (a g)")
                link(nc.vector.tensor_tensor(st_t[:, 0:GROUPS], st_m[:, 0:GROUPS], st_m[:, 0:GROUPS], ALU.mult))
                link(nc.vector.tensor_tensor(st_v[:, 0:GROUPS], st_v[:, 0:GROUPS], st_t[:, 0:GROUPS], ALU.subtract))
                link(nc.vector.tensor_tensor(st_v[:, 0:GROUPS], st_v[:, 0:GROUPS], sd0, ALU.mult))
                link(nc.vector.tensor_tensor(st_v[:, 0:GROUPS], st_v[:, 0:GROUPS], sd0, ALU.mult))
                nc.vector.tensor_scalar(st_v[:, 0:GROUPS], st_v[:, 0:GROUPS], 0.0, EPS, ALU.max, ALU.add).then_inc(var_made, 1)
                dve.wait_ge(sd_made, b * 2 + 3 if ahead else b * 2 + 2)
                link(nc.vector.reciprocal(st_v[:, 0:GROUPS], st_t[:, 0:GROUPS]))
                s1 = t_s1[:, bass.ds(b, 1), :].rearrange("p a g -> p (a g)")
                link(nc.vector.tensor_tensor(s1, st_v[:, 0:GROUPS], sd0, ALU.mult))
                link(nc.vector.tensor_tensor(t_s1m[:, bass.ds(b, 1), :].rearrange("p a g -> p (a g)"), s1,
                                             st_m[:, 0:GROUPS], ALU.mult))

            def image(b, ahead):
                with dve.Fori(0, CHUNKS) as j:
                    for r in range(ROWS):
                        row = b * H + j * ROWS + r
                        dve.wait_ge(qk_hi, row + 1)
                        src = acc[r % 4][:, 0:QK].rearrange("p (h c) -> p h c", h=HEADS)
                        nc.vector.tensor_tensor(qk[:, r % 4, :, 1, :], src, qk[:, r % 4, :, 0, :], ALU.subtract)\
                            .then_inc(qk_split, 1)
                        if ahead and r % 4 == 3:
                            stats_load(b + 1, j, r // 4)
                attention(b)
                if ahead:
                    stats_final(b + 1, b * 2 + 2)

                def z_lo(j, r):
                    pair = b * (H // 2) + j * PAIRS + r
                    dve.wait_ge(z_copied, 4 + pair + 1)
                    for i in range(2):
                        last = nc.vector.tensor_tensor(z_out[:, :, 2 * r + i, 1, :],
                                                       zf[:, r % 2, i * C:(i + 1) * C].rearrange("p (g c) -> p g c", c=CG),
                                                       z_out[:, :, 2 * r + i, 0, :], ALU.subtract)
                    last.then_inc(z_split, 1)

                for r in range(PAIRS):
                    z_lo(0, r)
                with dve.Fori(1, CHUNKS) as j:
                    for r in range(PAIRS):
                        z_lo(j, r)
                        if ahead and r < 2:
                            normalise_scale(b + 1, j - 1, r)
                        if ahead and r >= 1 and r < 3:
                            normalise_lo(b + 1, j - 1, r - 1)
                if ahead:
                    for slot in range(2):
                        normalise_scale(b + 1, CHUNKS - 1, slot)
                    for slot in range(2):
                        normalise_lo(b + 1, CHUNKS - 1, slot)
                    end_of_image(b + 1)
                z_final(b, ahead)

            with dve.Fori(0, CHUNKS) as j:
                for slot in range(2):
                    stats_load(0, j, slot)
            stats_final(0, 1)
            with dve.Fori(0, CHUNKS) as j:
                for slot in range(2):
                    normalise_scale(0, j, slot)
                    normalise_lo(0, j, slot)
            end_of_image(0)
            base = chain[1]
            with dve.Fori(0, B - 1) as b:
                chain[1] = 0
                chain[0] = b * LINKS + base
                image(b, True)
                assert chain[1] == LINKS, chain[1]
            chain[0] = (B - 1) * LINKS + base
            chain[1] = 0
            image(B - 1, False)

        layer0_block.close()
        layer0.close()
        stack.pop()
        layer1 = ctx.enter_context(ExitStack())
        stack.append(layer1)
        wide = sb("wide", [P, 2, CG, 2, W], f16)
        zin = sb("zin", [P, 2, H, 2, CG], f16)
        mixed_out = sb("mixed_out", [P, 2, CG, W])
        shift = sb("shift", [P, B, C])
        wsum = sb("wsum", [P, C])
        wsum_in = sb("wsum_in", [PIECES, C])
        bias_row = sb("bias_row", [P, C])
        held = sb("held", [PIECES, P])

        b_in = sem("b_in")
        held_made = sem("held_made")
        wsum_ps = sem("wsum_ps")
        shift_step = sem("shift_step")
        wide_in = [sem("wide_in0"), sem("wide_in1")]
        z_in = [sem("z_in0"), sem("z_in1")]
        quad_full = sem("quad_full")
        shifted = sem("shifted")
        quad_out = sem("quad_out")
        stored = sem("stored")
        out_free = sem("out_free")

        block1 = ctx.enter_context(nc.Block())

        @block1.sync
        def _(sp):
            sp.dma_start(wsum_in[:, :], wide_t).then_inc(b_in, 16)
            sp.dma_start(bias_row[:, :], bias.rearrange("(a c) -> a c", a=1).to_broadcast([P, C])).then_inc(b_in, 16)
            sp.wait_ge(held_made, 1)
            for g in range(CGROUPS):
                if g >= 2:
                    sp.wait_ge(quad_full, 2 * QUADS + (g - 1) * B * QUADS)
                sp.dma_start(wide[:, g % 2, :, :, :],
                             bass.AP(tensor=tab_dram.tensor, offset=g * CG * 4 * W + 1,
                                     ap=[[1, P], [4 * W, CG], [2 * W, 2], [1, W]])).then_inc(wide_in[g % 2], 16)
                with sp.Fori(0, B // 2) as i:
                    for s in range(2):
                        sp.wait_ge(quad_full, (g * B + i * 2 + s) * QUADS + QUADS)
                        sp.dma_start(zin[:, s, :, :, :].rearrange("p h s c -> p (h s c)"),
                                     z_dram[bass.ds(i * 2 + s, 1), :, g, :, :, :]
                                     .rearrange("b p h s c -> p (b h s c)")).then_inc(z_in[s], 16)

        @block1.gpsimd
        def _(pool):
            nc.gpsimd.memset(held[:, :], float(PIECE)).then_inc(held_made, 1)
            with pool.Fori(0, CGROUPS) as g:
                with pool.Fori(0, B // 2) as i:
                    for s in range(2):
                        pool.wait_ge(quad_out, 3 + (g * B + i * 2 + s) * QUADS + QUADS)
                        pool.dma_start(out[bass.ds(i * 2 + s, 1), bass.ds(g * CG, CG), :, :].rearrange("b c h w -> h (b c) w"),
                                       mixed_out[:, s, :, :]).then_inc(stored, 16)
                        pool.wait_ge(stored, (g * B + i * 2 + s + 1) * 16)
                        pool.sem_inc(out_free, 1)
            pool.wait_ge(stored, 16 * CGROUPS * B)

        @block1.tensor
        def _(pe):
            pe.sem_inc(quad_full, 2 * QUADS)
            pe.wait_ge(b_in, 32)
            pe.wait_ge(held_made, 1)
            nc.tensor.matmul(psum[7][:, 0:C], held[:, :], wsum_in[:, :], start=True, stop=True).then_inc(wsum_ps, 1)
            with pe.Fori(0, CGROUPS // 2) as gp:
                for gs_ in range(2):
                    pe.wait_ge(wide_in[gs_], (gp + 1) * 16)
                    pe.sem_inc(carried, 1)
                    with pe.Fori(0, B // 2) as i:
                        for s in range(2):
                            step = gp * (2 * B) + gs_ * B + i * 2 + s
                            pe.wait_ge(z_in[s], (gp * B + gs_ * (B // 2) + i + 1) * 16)
                            for q in range(QUADS):
                                pe.wait_ge(quad_out, step * QUADS + q + 1)
                                for k in range(QUAD):
                                    c = q * QUAD + k
                                    z_hi, z_lo = zin[:, s, :, 0, c], zin[:, s, :, 1, c]
                                    w_hi, w_lo = wide[:, gs_, c, 0, ::-1], wide[:, gs_, c, 1, ::-1]
                                    conv = psum[q % 3][:, k * W:(k + 1) * W]
                                    res = psum[3 + q % 3][:, k * W:(k + 1) * W]
                                    nc.tensor.matmul(conv, z_hi, w_hi, start=True, stop=False, skip_group_check=True)
                                    nc.tensor.matmul(conv, z_hi, w_lo, start=False, stop=False, skip_group_check=True)
                                    nc.tensor.matmul(res, z_hi, ident16[:, :], start=True, stop=False, skip_group_check=True)
                                    nc.tensor.matmul(conv, z_lo, w_hi, start=False, stop=True, skip_group_check=True)
                                    last = nc.tensor.matmul(res, z_lo, ident16[:, :], start=False, stop=True,
                                                            skip_group_check=True)
                                last.then_inc(quad_full, 1)

        @block1.scalar
        def _(act):
            act.wait_ge(shift_step, 1 + 3 * B)
            with act.Fori(0, CGROUPS) as g:
                with act.Fori(0, B // 2) as i:
                    for s in range(2):
                        step = g * B + i * 2 + s
                        act.wait_ge(out_free, step + 1)
                        sd = t_sd[:, bass.ds(i * 2 + s, 1), :].rearrange("p a g -> p (a g)")[:, bass.ds(g * (CG // GC), CG // GC)]
                        sh = shift[:, bass.ds(i * 2 + s, 1), :].rearrange("p a c -> p (a c)")[:, bass.ds(g * CG, CG)]
                        for q in range(QUADS):
                            act.wait_ge(quad_full, step * QUADS + 2 * QUADS + q + 1)
                            for k in range(QUAD):
                                c = q * QUAD + k
                                last = nc.scalar.activation(mixed_out[:, s, c, :], psum[3 + q % 3][:, k * W:(k + 1) * W],
                                                            ACT.Identity, scale=sd[:, c // GC:c // GC + 1],
                                                            bias=sh[:, c:c + 1])
                            last.then_inc(shifted, 1)

        @block1.vector
        def _(dve):
            dve.sem_inc(quad_out, 3)
            dve.sem_inc(out_free, 2)
            dve.wait_ge(wsum_ps, 1)
            nc.vector.tensor_copy(wsum[:, :], psum[7][:, 0:C]).then_inc(shift_step, 1)
            for b in range(B):
                def wide_row(t):
                    return t[:, b, :].rearrange("p (g a) -> p g a", a=1).to_broadcast([P, GROUPS, GC])

                row = shift[:, b, :].rearrange("p (g c) -> p g c", c=GC)
                dve.wait_ge(shift_step, 1 + 3 * b)
                nc.vector.tensor_tensor(row, wsum[:, :].rearrange("p (g c) -> p g c", c=GC), wide_row(t_s1m), ALU.mult)\
                    .then_inc(shift_step, 1)
                dve.wait_ge(shift_step, 2 + 3 * b)
                nc.vector.tensor_tensor(row, wide_row(t_mean), row, ALU.subtract).then_inc(shift_step, 1)
                dve.wait_ge(shift_step, 3 + 3 * b)
                nc.vector.tensor_tensor(shift[:, b, :], shift[:, b, :], bias_row[:, :], ALU.add).then_inc(shift_step, 1)
            with dve.Fori(0, CGROUPS) as g:
                with dve.Fori(0, B // 2) as i:
                    for s in range(2):
                        step = g * B + i * 2 + s
                        sc = t_s1[:, bass.ds(i * 2 + s, 1), :].rearrange("p a g -> p (a g)")[:, bass.ds(g * (CG // GC), CG // GC)]
                        for q in range(QUADS):
                            dve.wait_ge(shifted, step * QUADS + q + 1)
                            for k in range(QUAD):
                                c = q * QUAD + k
                                last = nc.vector.scalar_tensor_tensor(mixed_out[:, s, c, :], psum[q % 3][:, k * W:(k + 1) * W],
                                                                      sc[:, c // GC:c // GC + 1], mixed_out[:, s, c, :],
                                                                      ALU.mult, ALU.add)
                            last.then_inc(quad_out, 1)


def kernel(**inputs):
    import numpy as np
    import concourse.bacc as bacc
    from concourse import mybir
    from concourse.bass_utils import run_bass_kernel_spmd

    a = {k: np.asarray(v) for k, v in inputs.items()}
    order = np.concatenate([np.concatenate([np.arange(h * HC, (h + 1) * HC), C + np.arange(h * HC, (h + 1) * HC)])
                            for h in range(HEADS)])
    w_qkv, w_dw = a["L0_conv_w_qkv"], a["L0_conv_w_dw"].reshape(3 * C, TAPS)
    wide = a["L1_conv_weights"].reshape(C, PIECES)
    ch = np.arange(C)
    same = (ch[:, None] // GC == ch[None, :] // GC).astype(np.float32)
    cols = np.concatenate([ch[:CA], ch[CA:], ch[CA:]])
    arrays = {
        "x": a["x"],
        "w_qk": w_qkv[order].T, "w_v": w_qkv[2 * C:],
        "w_dw_qk": w_dw[order].T, "w_dw_v": w_dw[2 * C:],
        "w_proj_t": a["L0_conv_w_proj"].T, "temperature": a["L0_conv_temperature"].reshape(HEADS),
        "wide_w": wide, "wide_t": wide.T, "bias": a["L1_conv_bias"],
        "group_a": same[:CA][:, cols] / np.float32(GC),
        "group_b": same[np.concatenate([ch[CA:], ch[CA:]])][:, cols] / np.float32(2 * GC),
        "ident": np.eye(P, dtype=np.float32),
        "res_eye": np.float32(UP) * np.stack([np.eye(C, dtype=np.float32)[:CA],
                                              np.eye(C, dtype=np.float32)[np.concatenate([ch[CA:], ch[CA:]])]], axis=1),
    }
    nc = bacc.Bacc("TRN2", target_bir_lowering=False, num_devices=1)
    arrays = {f"in_{k}": np.ascontiguousarray(v) for k, v in arrays.items()}
    args = [nc.dram_tensor(k, v.shape, mybir.dt.from_np(v.dtype), kind="ExternalInput").ap() for k, v in arrays.items()]
    out = nc.dram_tensor("out", [B, C, H, W], mybir.dt.float32, kind="ExternalOutput").ap()
    conv_kernel(nc, *args, out)
    result = run_bass_kernel_spmd(nc, [arrays], core_ids=[0])
    return result.results[0]["out"]
```

```python
import concourse.bass as bass
from concourse import mybir
from contextlib import ExitStack

B, C, H, W = 8, 192, 128, 128
HEADS, HC = 4, 48
GROUPS, GC = 32, 6
TAPS = 9
PIECES, PIECE = 16, 8
EPS = 1e-5
NORM_EPS = 1e-12

P = 128
CA = 128
CB = C - CA
PITCH = W + 1
IMAGE = (H + 2) * PITCH + 1
ROWS = 8
CHUNKS = H // ROWS
STEP = ROWS * PITCH
WINDOW = (ROWS + 2) * PITCH + 1
LOAD_ROWS = 4
LOADS = H // LOAD_ROWS
NLOAD = LOAD_ROWS * W
QK = 2 * C
HQK = 2 * HC
PAIRS = ROWS // 2
TR, TC, TG = 8, 16, 24
TOUT = TR - 2
BAND = TC * TOUT
TILES = -(-H // TOUT)
WP = W + 2
Y_ROWS = (TILES - 1) * TOUT + TR
GPB = 4
BANKS_T = TG // GPB
OT = QK // P
UNITS = 2 * OT
S_SLOTS = (0, 1, 0)
S_ITER = len(S_SLOTS)
LOADS_PER = [S_SLOTS.count(s) * (TILES // 2 - 1) + 1 + CHUNKS for s in range(2)]
UP = 64.0
N_GROUP = GC * H * W
CG = 24
CGROUPS = C // CG
QUAD = 4
QUADS = CG // QUAD


def conv_kernel(nc, x, w_qk, w_v, w_dw_qk, masks_in, w_dw_v, w_proj_t, temperature, wide_w, wide_t, bias,
                group_a, group_b, ident_in, res_eye_in, out):
    f32, f16 = mybir.dt.float32, mybir.dt.float16
    ALU = mybir.AluOpType
    ACT = mybir.ActivationFunctionType
    AX = mybir.AxisListType

    ctx = ExitStack()
    with ctx:
        def sb(name, shape, dt=f32):
            return stack[-1].enter_context(nc.sbuf_tensor(name, shape, dt))

        def sem(name):
            return ctx.enter_context(nc.semaphore(name))

        stack = [ctx]
        z_dram = nc.dram_tensor("z_scratch", [B, P, CGROUPS, H, 2, CG], f16).ap()
        y_dram = nc.dram_tensor("y_scratch", [Y_ROWS, QK, 2, WP], f16).ap()
        tab_dram = nc.dram_tensor("wide_table", [C, 2, 2 * W], f16).ap()

        t_mean = sb("t_mean", [P, B, GROUPS])
        t_sd = sb("t_sd", [P, B, GROUPS])
        t_s1 = sb("t_s1", [P, B, GROUPS])
        t_s1m = sb("t_s1m", [P, B, GROUPS])
        ident = sb("ident", [P, P])
        ident16 = sb("ident16", [P, P], f16)
        ones = sb("ones", [P, P])

        psum = [ctx.enter_context(nc.psum_tensor(f"bank{i}", [P, 512], f32)) for i in range(8)]
        acc, gram, misc = psum[0:4], psum[4:6], psum[6:8]

        layer0 = ExitStack()
        layer0_block = ExitStack()
        stack.append(layer0)
        xa_hi = sb("xa_hi", [P, IMAGE], f16)
        xa_lo = sb("xa_lo", [P, IMAGE], f16)
        xb = sb("xb", [P, IMAGE], f16)
        w1 = sb("w1", [P, 2, 2, QK], f16)
        bands = sb("bands", [P, 2, TG, 3, BAND], f16)
        e_v = sb("e_v", [P, 2, 2, TAPS, C], f16)
        qk = sb("qk", [P, TOUT, 2, QK], f16)
        stage = sb("stage", [P, 2, 2, NLOAD])
        stage_hi = sb("stage_hi", [P, NLOAD], f16)
        space = sb("space", [P, 6576])

        def view(at, parts, shape, dt=f32):
            size = 4 if dt == f32 else 2
            n = 1
            for k in shape:
                n *= k
            v = space[0:parts, at // 4:(at + n * size) // 4]
            if dt != f32:
                v = v.bitcast(dt)
            names = " ".join(f"d{i}" for i in range(len(shape)))
            return v.rearrange(f"p ({names}) -> p {names}", **{f"d{i}": k for i, k in enumerate(shape)})

        Y2_BYTES = TG * 2 * WP * 2
        y2 = [view(s * Y2_BYTES, P, [TG, 2, WP], f16) for s in range(2)]
        gs = view(0, HQK, [HEADS, 2 * HQK])
        gg = view(3072, HQK, [HEADS, HQK])
        gt = view(4608, HQK, [HEADS, HQK])
        kn = view(6144, HC, [HEADS, HC])
        attn = view(6912, HC, [HEADS, HC])
        mt = view(7680, HC, [HEADS, C])
        dm = view(10752, HC, [2, HEADS, C])
        esum = view(16896, P, [2, C])
        wv = view(18432, HC, [HEADS, 2, P])
        wpt = view(22528, HC, [HEADS, C])
        colb = view(0, P, [2, 2, P])
        z_out = view(0, P, [CGROUPS, ROWS, 2, CG], f16)
        zf = view(6144, P, [2, 2 * C])
        sum_z = view(9216, P, [2 * C])
        sum_q = view(10752, P, [2 * C])
        sq = view(12288, P, [2 * C])
        ystage = view(13824, P, [2, OT, LOAD_ROWS, 2, WP], f16)
        table = view(0, HQK, [2, 2, 2 * W], f16)
        wide_tmp = view(4096, HQK, [2, PIECES])
        band_sum = view(7680, P, [TG, BAND])
        band_tmp = view(7680 + TG * BAND * 4, P, [TG, BAND])
        grp_a = sb("grp_a", [P, 2 * P])
        grp_b = sb("grp_b", [P, 2 * P])
        res_eye = sb("res_eye", [P, 2, C])
        wdv = sb("wdv", [HC, HEADS, TAPS])
        temp = sb("temp", [HC, HEADS])
        stats = sb("stats", [P, 2, LOADS, 6])
        mv = sb("mv", [P, 2, 2])
        col = sb("col", [P, 2, 2])
        st_m = sb("st_m", [P, GROUPS + 2])
        st_v = sb("st_v", [P, GROUPS + 2])
        st_t = sb("st_t", [P, GROUPS + 2])
        nbias = sb("nbias", [P, 2])
        r0up = sb("r0up", [P, C])
        small = sb("small", [HC, HEADS])
        qn = sb("qn", [HC, HEADS])
        wcol = stage[:, 0, 0, 0:TG * TAPS].rearrange("p (g t) -> p g t", g=TG)
        masks = stage[:, 0, 1, 0:3 * BAND].rearrange("p (d n) -> p d n", d=3)
        zeros = xa_hi[:, 0:P]

        carried = sem("carried")
        const_loaded = sem("const_loaded")
        loaded = [sem("loaded0"), sem("loaded1")]
        stats_used = sem("stats_used")
        w1_made = sem("w1_made")
        band_step = sem("band_step")
        bands_made = sem("bands_made")
        y_zeroed = sem("y_zeroed")
        borders = sem("borders")
        y_full = sem("y_full")
        y_hi = sem("y_hi")
        y_split = sem("y_split")
        y_stored = sem("y_stored")
        y2_loaded = [sem("y2_loaded0"), sem("y2_loaded1")]
        tile_full = sem("tile_full")
        attn_loaded = sem("attn_loaded")
        pads_zero = sem("pads_zero")
        taps_in = sem("taps_in")
        consts_made = sem("consts_made")
        table_made = sem("table_made")
        table_stored = sem("table_stored")
        affine = sem("affine")
        hi_made = sem("hi_made")
        normed = sem("normed")
        acc_full = sem("acc_full")
        qk_hi = sem("qk_hi")
        qk_split = sem("qk_split")
        gram_tiles = sem("gram_tiles")
        z_copied = sem("z_copied")
        z_split = sem("z_split")
        z_summed = sem("z_summed")
        z_stored = sem("z_stored")
        sums_zero = sem("sums_zero")
        pool_step = sem("pool_step")
        zsum_ps = sem("zsum_ps")
        zsum_read = sem("zsum_read")
        st_read = sem("st_read")
        step_v = sem("step_v")
        st_col = sem("st_col")
        st_ps = sem("st_ps")
        var_made = sem("var_made")
        sd_made = sem("sd_made")
        gram_copied = sem("gram_copied")
        gram_closed = sem("gram_closed")
        gram_t = sem("gram_t")
        diag_made = sem("diag_made")
        colsum = sem("colsum")
        norms_ready = sem("norms_ready")
        norms_rooted = sem("norms_rooted")
        logits = sem("logits")
        exped = sem("exped")
        attn_made = sem("attn_made")
        mt_ps = sem("mt_ps")
        dm_made = sem("dm_made")
        e_ps = sem("e_ps")
        e_sum = sem("e_sum")
        e_hi = sem("e_hi")
        e_lo = sem("e_lo")

        def settled(engine):
            engine.sem_inc(carried, 1)

        def block_of(i):
            return (xa_hi, xa_lo, xb)[i]

        def body_rows(tensor, chunk, first):
            win = tensor[:, bass.ds(chunk * STEP, WINDOW)]
            v = win[:, 0:(ROWS + 2) * PITCH].rearrange("p (r c) -> p r c", c=PITCH)
            return v[:, 1 + first:1 + first + LOAD_ROWS, 1:1 + W]

        def t_bank(half, t):
            return (half * OT + t) % 2

        def tile_in(s, q):
            return acc[(s * BANKS_T + q) % 4][:, 0:GPB * BAND].rearrange("p (g r c) -> p r c g", r=TOUT, c=TC)

        def tile_out(q, low):
            return qk[:, :, low, :].rearrange("p r (c g) -> p r c g", g=TG)[:, :, :, q * GPB:(q + 1) * GPB]

        def rows(ap):
            return ap.rearrange("p (r c) -> p r c", c=W)

        PRODUCTS = [(0, 0, 0), (0, 1, 0), (1, 0, 0), (2, 0, 1), (2, 1, 1)]
        N_CONST = 12
        U_IMG = CHUNKS * UNITS

        block = layer0_block.enter_context(nc.Block())

        @block.sync
        def _(sp):
            for dst, src in (
                (grp_a[:, :], group_a), (grp_b[:, :], group_b), (ident[:, :], ident_in),
                (res_eye[:, :, :], res_eye_in),
                (wdv[:, :, :], w_dw_v.rearrange("(h p) t -> p h t", p=HC)),
                (temp[:, :], temperature.rearrange("(a h) -> a h", a=1).to_broadcast([HC, HEADS])),
                (stage[:, 1, 0, 0:QK], w_qk[0:CA, :]),
                (stage[0:CB, 1, 1, 0:QK], w_qk[CA:C, :]),
                (stage[CB:P, 1, 1, 0:QK], w_qk[CA:C, :]),
                (masks, masks_in),
                (wide_tmp[:, 0, :], wide_w[0:HQK, :]), (wide_tmp[:, 1, :], wide_w[HQK:C, :]),
            ):
                sp.dma_start(dst, src).then_inc(const_loaded, 16)
            for r in range(TR):
                sp.dma_start(stage[r * TC:(r + 1) * TC, 0, 0, 0:TG * TAPS], w_dw_qk).then_inc(taps_in, 16)
            sp.wait_ge(pads_zero, 1)
            for r in [0, *range(H + 1, Y_ROWS)]:
                sp.dma_start(y_dram[r, :, :, :].rearrange("(t p) s w -> p t (s w)", p=P),
                             xa_hi[:, 0:OT * 2 * WP].rearrange("p (t n) -> p t n", t=OT)).then_inc(y_zeroed, 16)
            sp.wait_ge(table_made, 2)
            for part in range(2):
                sp.dma_start(tab_dram[part * HQK:(part + 1) * HQK, :, :], table[:, part, :, :]).then_inc(table_stored, 16)
            sp.wait_ge(w1_made, 1)
            sp.wait_ge(bands_made, 1)

            def load(b, r0, slot, blocks=3):
                for dst, c0, c1 in ((stage[:, slot, 0, :], 0, CA), (stage[0:CB, slot, 1, :], CA, C),
                                    (stage[CB:P, slot, 1, :], CA, C))[0:blocks]:
                    sp.dma_start(dst, x[bass.ds(b, 1), c0:c1, bass.ds(r0, LOAD_ROWS), :].rearrange("b c h w -> c (b h w)"))\
                        .then_inc(loaded[slot], 16)

            def load_to_normalise(b, j):
                for slot in range(2):
                    sp.wait_ge(normed, b * LOADS + j * 2 + slot + 1)
                    settled(sp)
                    load(b, j * ROWS + slot * LOAD_ROWS, slot)

            def store_z(b, j):
                sp.wait_ge(z_split, 1 + b * (H // 2) + j * PAIRS + PAIRS)
                sp.dma_start(z_dram[bass.ds(b, 1), :, :, bass.ds(j * ROWS, ROWS), :, :].rearrange("b p g r s c -> p (b g) (r s c)"),
                             z_out[:, :, :, :, :].rearrange("p g r s c -> p g (r s c)")).then_inc(z_stored, 16)

            def store_y(b, j):
                for half in range(2):
                    for t in range(OT):
                        u = (b * CHUNKS + j) * UNITS + half * OT + t
                        sp.wait_ge(y_split, 2 + u + 1)
                        sp.dma_start(y_dram[bass.ds(j * ROWS + half * LOAD_ROWS + 1, LOAD_ROWS), t * P:(t + 1) * P, :, :]
                                     .rearrange("r p s w -> p r (s w)"),
                                     ystage[:, half, t, :, :, :].rearrange("p r s w -> p r (s w)")).then_inc(y_stored, 16)

            def load_tiles(b, it, ahead, n_stats):
                for s in range(2):
                    k = it * 2 + s
                    sp.wait_ge(tile_full, (b * TILES + k + 1) * BANKS_T)
                    sp.dma_start(y2[s].rearrange("p g s w -> p (g s w)"),
                                 y_dram[bass.ds(k * TOUT, TR), :, :, :].rearrange("r (c g) s w -> (r c) (g s w)", c=TC))\
                        .then_inc(y2_loaded[s], 16)
                if ahead:
                    for i in range(n_stats):
                        sp.wait_ge(stats_used, (b + 1) * LOADS + it * S_ITER + (i + 1 if i else 2))
                        load(b + 1, (it * S_ITER + i) * LOAD_ROWS, S_SLOTS[i], 2)

            def image(b, ahead):
                sp.wait_ge(zsum_ps, 1 + b)
                sp.wait_ge(z_stored, 16 + b * CHUNKS * 16)
                sp.wait_ge(y_stored, 96 + (b + 1) * CHUNKS * 96)
                sp.wait_ge(normed, 2 + (b + 1) * LOADS)
                settled(sp)
                with sp.Fori(0, TILES // 2 - 1) as it:
                    load_tiles(b, it, ahead, S_ITER)
                load_tiles(b, TILES // 2 - 1, ahead, 2)
                sp.wait_ge(gram_closed, b + 1)
                sp.dma_start(wv.rearrange("p h i m -> p (h i m)"), w_v).then_inc(attn_loaded, 16)
                sp.dma_start(wpt, w_proj_t.rearrange("(h p) o -> p h o", p=HC)).then_inc(attn_loaded, 16)
                if ahead:
                    sp.wait_ge(stats_used, 2 + (b + 2) * LOADS)
                    settled(sp)
                    load_to_normalise(b + 1, 0)
                store_z(b, 0)
                with sp.Fori(1, CHUNKS) as j:
                    if ahead:
                        load_to_normalise(b + 1, j)
                    store_z(b, j)
                    if ahead:
                        store_y(b + 1, j - 1)
                if ahead:
                    store_y(b + 1, CHUNKS - 1)

            with sp.Fori(0, CHUNKS) as j:
                for slot in range(2):
                    sp.wait_ge(stats_used, j * 2 + slot + 1)
                    load(0, j * ROWS + slot * LOAD_ROWS, slot, 2)
            sp.wait_ge(stats_used, 2 + LOADS)
            load_to_normalise(0, 0)
            with sp.Fori(1, CHUNKS) as j:
                load_to_normalise(0, j)
                store_y(0, j - 1)
            store_y(0, CHUNKS - 1)
            sp.wait_ge(y_zeroed, 16 * (Y_ROWS - H))
            with sp.Fori(0, B - 1) as b:
                image(b, True)
            image(B - 1, False)
            sp.wait_ge(z_stored, 16 + 16 * B * CHUNKS)
            sp.wait_ge(table_stored, 32)

        @block.gpsimd
        def _(pool):
            for t in (xa_hi, xa_lo, xb):
                nc.gpsimd.memset(t[:, :], 0.0).then_inc(pads_zero, 1)
            nc.gpsimd.memset(ones[:, :], 1.0).then_inc(pads_zero, 1)
            pool.wait_ge(const_loaded, 16 * N_CONST)
            pool.wait_ge(taps_in, 16 * TR)
            n = 0

            def after(ins):
                nonlocal n
                n += 1
                ins.then_inc(band_step, 1)
                pool.wait_ge(band_step, n)

            for dx in range(3):
                for dy in range(3):
                    mask = masks[:, dy:dy + 1, :].to_broadcast([P, TG, BAND])
                    tap = wcol[:, :, dy * 3 + dx:dy * 3 + dx + 1].to_broadcast([P, TG, BAND])
                    after(nc.gpsimd.tensor_tensor(band_tmp if dy else band_sum, mask, tap, ALU.mult))
                    if dy:
                        after(nc.gpsimd.tensor_tensor(band_sum, band_sum, band_tmp, ALU.add))
                after(nc.gpsimd.tensor_copy(bands[:, 0, :, dx, :], band_sum))
                after(nc.gpsimd.tensor_tensor(bands[:, 1, :, dx, :], band_sum, bands[:, 0, :, dx, :], ALU.subtract))
            pool.sem_inc(bands_made, 1)

            def clear_borders(n):
                for side in (0, WP - 1):
                    nc.gpsimd.memset(ystage.rearrange("p h t r s w -> p (h t r s) w")[:, :, side:side + 1], 0.0)\
                        .then_inc(borders, 1)

            clear_borders(0)
            with pool.Fori(0, B) as b:
                pool.wait_ge(e_lo, 1 + b * TAPS + TAPS)
                settled(pool)
                nc.gpsimd.memset(sum_z[:, :], 0.0).then_inc(sums_zero, 1)
                nc.gpsimd.memset(sum_q[:, :], 0.0).then_inc(sums_zero, 1)
                clear_borders(b + 1)
                pool.wait_ge(sums_zero, b * 2 + 2)
                settled(pool)
                with pool.Fori(0, H // 4) as j:
                    for s in range(2):
                        n = b * (H // 2) + j * 2 + s
                        pool.wait_ge(z_copied, 4 + n + 1)
                        pool.wait_ge(z_summed, 1 + n)
                        nc.gpsimd.tensor_tensor(sq[:, :], zf[:, s, :], zf[:, s, :], ALU.mult).then_inc(pool_step, 1)
                        nc.gpsimd.tensor_tensor(sum_z[:, :], sum_z[:, :], zf[:, s, :], ALU.add).then_inc(pool_step, 1)
                        pool.wait_ge(pool_step, n * 2 + 2)
                        nc.gpsimd.tensor_tensor(sum_q[:, :], sum_q[:, :], sq[:, :], ALU.add).then_inc(z_summed, 1)

        @block.scalar
        def _(act):
            act.wait_ge(const_loaded, 16 * N_CONST)
            nc.scalar.activation(ident16[:, :], ident[:, :], ACT.Copy).then_inc(consts_made, 1)

            def normalise_hi(b, j, slot):
                n = b * LOADS + j * 2 + slot
                act.wait_ge(affine, n * 2 + 2)
                nc.scalar.activation(body_rows(xa_hi, j, slot * LOAD_ROWS), rows(stage[:, slot, 0, :]), ACT.Copy)\
                    .then_inc(hi_made, 1)
                nc.scalar.activation(body_rows(xb, j, slot * LOAD_ROWS)[0:CB], rows(stage[0:CB, slot, 1, :]), ACT.Copy)\
                    .then_inc(hi_made, 1)
                act.wait_ge(normed, 2 + b * LOADS + j * 2 + slot)
                nc.scalar.activation(stage_hi[CB:P, :], stage[CB:P, slot, 1, :], ACT.Copy).then_inc(hi_made, 1)

            def root(n, width):
                act.wait_ge(var_made, n)
                nc.scalar.activation(st_t[:, 0:width], st_v[:, 0:width], ACT.Sqrt).then_inc(sd_made, 1)

            def y_high(b, j):
                act.wait_ge(y_stored, 96 + (b * CHUNKS + j) * 96)
                for half in range(2):
                    for t in range(OT):
                        u = (b * CHUNKS + j) * UNITS + half * OT + t
                        act.wait_ge(y_full, u + 1)
                        nc.scalar.activation(ystage[:, half, t, :, 0, 1:1 + W], rows(gram[t_bank(half, t)][:, :]), ACT.Copy)\
                            .then_inc(y_hi, 1)

            def tiles(b, it):
                for s in range(2):
                    k = b * TILES + it * 2 + s
                    act.wait_ge(gram_tiles, k + 1)
                    for q in range(BANKS_T):
                        act.wait_ge(tile_full, 2 * BANKS_T + k * BANKS_T + q + 1)
                        nc.scalar.activation(tile_out(q, 0), tile_in(s, q), ACT.Copy).then_inc(qk_hi, 1)

            def z_pair(b, j, r):
                pair = b * (H // 2) + j * PAIRS + r
                act.wait_ge(acc_full, b * (H // 2) + j * PAIRS + r + 1)
                if r == 0:
                    act.wait_ge(z_stored, 16 + (b * CHUNKS + j) * 16)
                act.wait_ge(z_split, 1 + pair)
                act.wait_ge(z_summed, 1 + pair)
                for i in range(2):
                    nc.scalar.activation(z_out[:, :, 2 * r + i, 0, :],
                                         acc[r % 4][:, i * C:(i + 1) * C].rearrange("p (g c) -> p g c", c=CG),
                                         ACT.Copy, scale=1.0 / UP)
                nc.scalar.activation(zf[:, r % 2, :], acc[r % 4][:, 0:2 * C], ACT.Copy, scale=1.0 / UP)\
                    .then_inc(z_copied, 1)

            def attention(b):
                act.wait_ge(norms_ready, b * 2 + 2)
                nc.scalar.activation(kn[:, :, :], gt[0:HC, :, HC:HQK], ACT.Sqrt).then_inc(norms_rooted, 1)
                nc.scalar.activation(qn[:, :], small[:, :], ACT.Sqrt).then_inc(norms_rooted, 1)
                act.wait_ge(logits, b + 1)
                nc.scalar.activation(gt[0:HC, :, 0:HC], attn[:, :, :], ACT.Exp).then_inc(exped, 1)
                for t in range(TAPS):
                    act.wait_ge(e_sum, b * TAPS + t + 1)
                    nc.scalar.activation(e_v[:, 0, :, t, :], esum[:, :, :], ACT.Copy).then_inc(e_hi, 1)

            def image(b, ahead):
                with act.Fori(0, TILES // 2) as it:
                    tiles(b, it)
                attention(b)
                if ahead:
                    root(b * 2 + 2, GROUPS + 2)
                    act.wait_ge(borders, 2 * (b + 2))
                for r in range(PAIRS):
                    z_pair(b, 0, r)
                with act.Fori(1, CHUNKS) as j:
                    for r in range(PAIRS):
                        z_pair(b, j, r)
                        if ahead and r >= 1 and r < 3:
                            normalise_hi(b + 1, j - 1, r - 1)
                    if ahead:
                        y_high(b + 1, j - 1)
                if ahead:
                    for slot in range(2):
                        normalise_hi(b + 1, CHUNKS - 1, slot)
                    y_high(b + 1, CHUNKS - 1)
                root(b * 2 + 3 if ahead else b * 2 + 2, GROUPS)

            act.wait_ge(pads_zero, 4)
            act.wait_ge(y_zeroed, 16 * (Y_ROWS - H))
            root(1, GROUPS + 2)
            act.wait_ge(borders, 2)
            with act.Fori(0, CHUNKS) as j:
                for slot in range(2):
                    normalise_hi(0, j, slot)
                y_high(0, j)
            act.wait_ge(table_stored, 32)
            with act.Fori(0, B - 1) as b:
                image(b, True)
            image(B - 1, False)

        @block.tensor
        def _(pe):
            def row_products(bank, base, weights, n, win, r):
                k = 0
                for t in range(TAPS):
                    at = (r + t // 3) * PITCH + t % 3
                    for blk, half, wblk in PRODUCTS:
                        last = nc.tensor.matmul(bank[:, base:base + n], win[blk][:, at:at + W],
                                                weights[:, half, wblk, t, :], start=k == 0,
                                                stop=k == TAPS * len(PRODUCTS) - 1, skip_group_check=True)
                        k += 1
                return last

            def pointwise(b, j):
                pe.wait_ge(normed, 2 + b * LOADS + j * 2 + 2)
                for half in range(2):
                    win = [body_rows(block_of(i), j, half * LOAD_ROWS) for i in range(3)]
                    for t in range(OT):
                        u = (b * CHUNKS + j) * UNITS + half * OT + t
                        pe.wait_ge(y_split, u + 1)
                        for k, (blk, low, wblk) in enumerate(PRODUCTS):
                            last = nc.tensor.matmul(gram[t_bank(half, t)][:, :], w1[:, low, wblk, t * P:(t + 1) * P], win[blk],
                                                    start=k == 0, stop=k == len(PRODUCTS) - 1, skip_group_check=True)
                        last.then_inc(y_full, 1)

            def taps(b, it, s, banks):
                k = b * TILES + it * 2 + s
                for q in banks:
                    pe.wait_ge(qk_split, k * BANKS_T + q + 1)
                    for i in range(GPB):
                        g = q * GPB + i
                        n = 0
                        for dx in range(3):
                            for y_low, w_low in ((0, 0), (0, 1), (1, 0)):
                                last = nc.tensor.matmul(acc[(s * BANKS_T + q) % 4][:, i * BAND:(i + 1) * BAND],
                                                        y2[s][:, g, y_low, dx:dx + W], bands[:, w_low, g, dx, :],
                                                        start=n == 0, stop=n == 8, skip_group_check=True)
                                n += 1
                    last.then_inc(tile_full, 1)

            def gram_tile(b, it, s, n_rows):
                k = b * TILES + it * 2 + s
                pe.wait_ge(qk_split, 4 + k * BANKS_T + BANKS_T)
                for r in range(n_rows):
                    for h in range(HEADS):
                        at = (h % 2) * 2 * HQK
                        last = nc.tensor.matmul(gram[h // 2][0:HQK, at:at + 2 * HQK], qk[:, r, 0, h * HQK:(h + 1) * HQK],
                                                qk[:, r, :, h * HQK:(h + 1) * HQK], start=False, stop=False,
                                                skip_group_check=True)
                last.then_inc(gram_tiles, 1)

            def tile_pair(b, it, last_rows):
                for s in range(2):
                    pe.wait_ge(y2_loaded[s], (b * (TILES // 2) + it + 1) * 16)
                    if s:
                        taps(b, it, 1, range(2))
                        gram_tile(b, it, 0, TOUT)
                        taps(b, it, 1, range(2, BANKS_T))
                    else:
                        taps(b, it, 0, range(BANKS_T))
                gram_tile(b, it, 1, last_rows)

            def gram_edge(first):
                for g in gram:
                    for i in range(QK // P):
                        last = nc.tensor.matmul(g[0:HQK, i * P:(i + 1) * P], zeros[:, 0:HQK], zeros,
                                                start=first and i == 0, stop=not first, skip_group_check=True)
                return last

            def windows(j):
                return [block_of(i)[:, bass.ds(j * STEP, WINDOW)] for i in range(3)]

            def stats_sums(n):
                pe.wait_ge(st_col, n)
                for s in range(2):
                    for i, g in enumerate((grp_a, grp_b)):
                        nc.tensor.matmul(misc[0][:, s * C:(s + 1) * C], colb[:, i, s, :], g[:, 0:C],
                                         start=i == 0, stop=i == 1, skip_group_check=True)
                for m in range(2):
                    for i, g in enumerate((grp_a, grp_b)):
                        last = nc.tensor.matmul(misc[1][:, 2 * m:2 * m + 2], g[:, m * P:(m + 1) * P], col[:, i, :],
                                                start=i == 0, stop=i == 1, skip_group_check=True)
                last.then_inc(st_ps, 1)

            def image(b, ahead):
                pe.wait_ge(z_copied, 4 + b * (H // 2))
                pe.wait_ge(y_split, 2 + (b + 1) * U_IMG)
                gram_edge(True)
                with pe.Fori(0, TILES // 2 - 1) as it:
                    tile_pair(b, it, TOUT)
                tile_pair(b, TILES // 2 - 1, H - (TILES - 1) * TOUT)
                gram_edge(False).then_inc(gram_closed, 1)
                pe.wait_ge(gram_copied, 2 + b * 2 + 2)
                pe.wait_ge(zsum_read, 1 + b)
                for h in range(HEADS):
                    last = nc.tensor.transpose(misc[0][0:HQK, h * HQK:(h + 1) * HQK], gs[:, h, HQK:2 * HQK],
                                               ident[0:HQK, 0:HQK])
                last.then_inc(gram_t, 1)
                pe.wait_ge(diag_made, b + 1)
                nc.tensor.matmul(misc[1][0:HQK, 0:QK], ones[0:HQK, 0:HQK], gt[:, :, :].rearrange("p h c -> p (h c)"),
                                 start=True, stop=True).then_inc(colsum, 1)
                pe.wait_ge(attn_loaded, 32 * (b + 1))
                pe.wait_ge(attn_made, b + 1)
                settled(pe)
                for h in range(HEADS):
                    last = nc.tensor.matmul(misc[h // 2][0:HC, (h % 2) * C:(h % 2 + 1) * C], attn[:, h, :], wpt[:, h, :],
                                            start=True, stop=True, skip_group_check=True)
                last.then_inc(mt_ps, 1)
                for t in range(TAPS):
                    pe.wait_ge(dm_made, b * TAPS + t + 1)
                    if t >= 2:
                        pe.wait_ge(e_sum, b * TAPS + t - 1)
                    for i in range(2):
                        for h in range(HEADS):
                            last = nc.tensor.matmul(misc[t % 2][:, i * C:(i + 1) * C], wv[:, h, i, :], dm[:, t % 2, h, :],
                                                    start=h == 0, stop=h == HEADS - 1, skip_group_check=True)
                    last.then_inc(e_ps, 1)
                if ahead:
                    pe.wait_ge(e_sum, b * TAPS + TAPS)
                    stats_sums(b + 2)
                pe.wait_ge(e_lo, 1 + b * TAPS + TAPS)
                settled(pe)
                def value_rows(j):
                    win = windows(j)
                    for r in range(PAIRS):
                        pe.wait_ge(z_copied, b * (H // 2) + j * PAIRS + r + 1)
                        row_products(acc[r], 0, e_v, C, win, 2 * r)
                        row_products(acc[r], C, e_v, C, win, 2 * r + 1).then_inc(acc_full, 1)

                value_rows(0)
                with pe.Fori(1, CHUNKS) as j:
                    value_rows(j)
                    if ahead:
                        pointwise(b + 1, j - 1)
                if ahead:
                    pointwise(b + 1, CHUNKS - 1)
                pe.wait_ge(z_summed, 1 + b * (H // 2) + H // 2)
                if ahead:
                    pe.wait_ge(st_read, b + 2)
                nc.tensor.matmul(misc[0][:, 0:2 * C], ones[:, :], sum_z[:, :], start=True, stop=True)
                nc.tensor.matmul(misc[1][:, 0:2 * C], ones[:, :], sum_q[:, :], start=True, stop=True).then_inc(zsum_ps, 1)

            pe.wait_ge(const_loaded, 16 * N_CONST)
            pe.wait_ge(pads_zero, 4)
            pe.wait_ge(w1_made, 1)
            stats_sums(1)
            with pe.Fori(0, CHUNKS) as j:
                pointwise(0, j)
            pe.wait_ge(bands_made, 1)
            with pe.Fori(0, B - 1) as b:
                image(b, True)
            image(B - 1, False)

        @block.vector
        def _(dve):
            chain = [0, 0]
            LINKS = 33

            def link(ins):
                chain[1] += 1
                ins.then_inc(step_v, 1)
                dve.wait_ge(step_v, chain[0] + chain[1])

            dve.wait_ge(const_loaded, 16 * N_CONST)
            for free, n in ((qk_split, 4), (z_copied, 4), (gram_tiles, 1), (stats_used, 2), (normed, 2), (gram_copied, 2),
                            (zsum_ps, 1), (zsum_read, 1), (z_summed, 1), (z_split, 1), (e_lo, 1), (z_stored, 16),
                            (y_split, 2), (y_stored, 96), (tile_full, 2 * BANKS_T)):
                dve.sem_inc(free, n)
            link(nc.vector.memset(mv[:, :, :], 0.0))
            for i in range(2):
                link(nc.vector.tensor_scalar(stage[:, 1, i, 0:QK], stage[:, 1, i, 0:QK], UP, None, ALU.mult))
                link(nc.vector.tensor_copy(w1[:, 0, i, :], stage[:, 1, i, 0:QK]))
                link(nc.vector.tensor_tensor(w1[:, 1, i, :], stage[:, 1, i, 0:QK], w1[:, 0, i, :], ALU.subtract))
            dve.sem_inc(w1_made, 1)
            for part in range(2):
                src = wide_tmp[:, part, :].rearrange("p (n c) -> p n c", c=1).to_broadcast([HQK, PIECES, PIECE])
                for a in range(2):
                    hi, lo = [table[:, part, s, a * W:(a + 1) * W].rearrange("p (n c) -> p n c", c=PIECE) for s in range(2)]
                    link(nc.vector.tensor_copy(hi, src))
                    link(nc.vector.tensor_tensor(lo, src, hi, ALU.subtract))
                dve.sem_inc(table_made, 1)

            def first_loads(slot, b1, loads3, loads2):
                n3, n2 = CHUNKS, S_SLOTS.count(slot) * (TILES // 2 - 1) + 1
                if b1 is None:
                    return 48 * loads3 + 32 * loads2
                return (48 + 32) * CHUNKS + b1 * (48 * n3 + 32 * n2) + 48 * loads3 + 32 * loads2

            def stats_load(slot, count, at):
                dve.wait_ge(loaded[slot], count)
                nc.vector.bn_stats(stats[:, 0, bass.ds(at, 1), :].rearrange("p a s -> p (a s)"), stage[:, slot, 0, :])
                nc.vector.bn_stats(stats[0:CB, 1, bass.ds(at, 1), :].rearrange("p a s -> p (a s)"), stage[0:CB, slot, 1, :])\
                    .then_inc(stats_used, 1)

            def stats_final(b, turn):
                dve.wait_ge(stats_used, 2 + b * LOADS + LOADS)
                settled(dve)
                nc.vector.bn_aggr(mv[:, 0, :], stats[:, 0, :, :].rearrange("p n s -> p (n s)"))
                link(nc.vector.bn_aggr(mv[0:CB, 1, :], stats[0:CB, 1, :, :].rearrange("p n s -> p (n s)")))
                nc.vector.tensor_copy(col[:, :, 0], mv[:, :, 0])
                link(nc.vector.tensor_tensor(col[:, :, 1], mv[:, :, 0], mv[:, :, 0], ALU.mult))
                link(nc.vector.tensor_tensor(col[:, :, 1], col[:, :, 1], mv[:, :, 1], ALU.add))
                nc.vector.tensor_copy(colb[:, :, :, :], col[:, :, :].rearrange("p i (s a) -> p i s a", a=1)
                                      .to_broadcast([P, 2, 2, P])).then_inc(st_col, 1)
                dve.wait_ge(st_ps, b + 1)
                sums = misc[0][:, 0:2 * C].rearrange("p (s g c) -> p s g c", s=2, c=GC)
                nc.vector.tensor_copy(st_m[:, 0:GROUPS], sums[:, 0, :, 0])
                nc.vector.tensor_copy(st_v[:, 0:GROUPS], sums[:, 1, :, 0])
                nc.vector.tensor_copy(st_m[:, GROUPS:], misc[1][:, 0:4:2])
                nc.vector.tensor_copy(st_v[:, GROUPS:], misc[1][:, 1:4:2]).then_inc(st_read, 1)
                dve.wait_ge(st_read, b + 1)
                link(nc.vector.tensor_tensor(st_t[:, :], st_m[:, :], st_m[:, :], ALU.mult))
                link(nc.vector.tensor_tensor(st_v[:, :], st_v[:, :], st_t[:, :], ALU.subtract))
                nc.vector.tensor_scalar(st_v[:, :], st_v[:, :], 0.0, EPS, ALU.max, ALU.add).then_inc(var_made, 1)
                dve.wait_ge(sd_made, turn)
                nc.vector.tensor_copy(t_sd[:, bass.ds(b, 1), :].rearrange("p a g -> p (a g)"), st_t[:, 0:GROUPS])
                nc.vector.tensor_copy(t_mean[:, bass.ds(b, 1), :].rearrange("p a g -> p (a g)"), st_m[:, 0:GROUPS])
                link(nc.vector.reciprocal(st_v[:, :], st_t[:, :]))
                nc.vector.scalar_tensor_tensor(nbias[:, :], st_m[:, GROUPS:], -1.0, st_v[:, GROUPS:], ALU.mult, ALU.mult)
                link(nc.vector.tensor_scalar(r0up[:, :].rearrange("p (g c) -> p g c", c=GC),
                                             st_v[:, 0:GROUPS].rearrange("p (g a) -> p g a", a=1).to_broadcast([P, GROUPS, GC]),
                                             UP, None, ALU.mult))

            def normalise_scale(b, j, slot, b1=None):
                n2 = CHUNKS if b1 is None else S_SLOTS.count(slot) * (TILES // 2 - 1) + 1
                dve.wait_ge(loaded[slot], first_loads(slot, b1, j + 1, n2))
                for i in range(2):
                    nc.vector.tensor_scalar(stage[:, slot, i, :], stage[:, slot, i, :], st_v[:, GROUPS + i:GROUPS + i + 1],
                                            nbias[:, i:i + 1], ALU.mult, ALU.add).then_inc(affine, 1)

            def normalise_lo(b, j, slot):
                n = b * LOADS + j * 2 + slot
                dve.wait_ge(hi_made, n * 3 + 3)
                first = slot * LOAD_ROWS
                nc.vector.tensor_tensor(body_rows(xa_lo, j, first), rows(stage[:, slot, 0, :]), body_rows(xa_hi, j, first),
                                        ALU.subtract)
                nc.vector.tensor_tensor(body_rows(xb, j, first)[CB:P], rows(stage[CB:P, slot, 1, :]), rows(stage_hi[CB:P, :]),
                                        ALU.subtract).then_inc(normed, 1)

            def y_low(b, j):
                for half in range(2):
                    for t in range(OT):
                        u = (b * CHUNKS + j) * UNITS + half * OT + t
                        dve.wait_ge(y_hi, u + 1)
                        nc.vector.tensor_tensor(ystage[:, half, t, :, 1, 1:1 + W], rows(gram[t_bank(half, t)][:, :]),
                                                ystage[:, half, t, :, 0, 1:1 + W], ALU.subtract).then_inc(y_split, 1)

            def attention(b):
                dve.wait_ge(gram_closed, b + 1)
                for g in range(2):
                    nc.vector.tensor_copy(gs[:, 2 * g:2 * g + 2, :], gram[g][0:HQK, 0:QK].rearrange("p (h c) -> p h c", h=2))\
                        .then_inc(gram_copied, 1)
                dve.wait_ge(gram_t, b + 1)
                dve.wait_ge(gram_copied, 2 + b * 2 + 2)
                link(nc.vector.tensor_tensor(gg[:, :, :], gs[:, :, 0:HQK], gs[:, :, HQK:2 * HQK], ALU.add))
                link(nc.vector.tensor_tensor(gg[:, :, :], misc[0][0:HQK, 0:QK].rearrange("p (h c) -> p h c", h=HEADS),
                                             gg[:, :, :], ALU.add))
                eye = ident[0:HQK, 0:HQK].rearrange("p (a c) -> p a c", a=1).to_broadcast([HQK, HEADS, HQK])
                nc.vector.tensor_tensor(gt[:, :, :], gg[:, :, :], eye, ALU.mult).then_inc(diag_made, 1)
                dve.wait_ge(diag_made, b + 1)
                link(nc.vector.tensor_reduce(small[:, :], gt[0:HC, :, 0:HC], AX.X, ALU.add))
                nc.vector.tensor_scalar(small[:, :], small[:, :], 0.0, None, ALU.max).then_inc(norms_ready, 1)
                dve.wait_ge(colsum, b + 1)
                nc.vector.tensor_scalar(gt[0:HC, :, HC:HQK],
                                        misc[1][0:HC, 0:QK].rearrange("p (h c) -> p h c", h=HEADS)[:, :, HC:HQK],
                                        0.0, None, ALU.max).then_inc(norms_ready, 1)
                dve.wait_ge(norms_rooted, b * 2 + 2)
                link(nc.vector.tensor_scalar(kn[:, :, :], kn[:, :, :], NORM_EPS * UP, None, ALU.max))
                link(nc.vector.tensor_scalar(qn[:, :], qn[:, :], NORM_EPS * UP, None, ALU.max))
                link(nc.vector.reciprocal(kn[:, :, :], kn[:, :, :]))
                link(nc.vector.reciprocal(qn[:, :], qn[:, :]))
                link(nc.vector.tensor_tensor(qn[:, :], qn[:, :], temp[:, :], ALU.mult))
                link(nc.vector.tensor_tensor(attn[:, :, :], gg[0:HC, :, HC:HQK], kn[:, :, :], ALU.mult))

                def over(t):
                    return t[:, :].rearrange("p (h a) -> p h a", a=1).to_broadcast([HC, HEADS, HC])

                link(nc.vector.tensor_tensor(attn[:, :, :], attn[:, :, :], over(qn), ALU.mult))
                link(nc.vector.tensor_reduce(small[:, :], attn[:, :, :], AX.X, ALU.max))
                nc.vector.tensor_tensor(attn[:, :, :], attn[:, :, :], over(small), ALU.subtract).then_inc(logits, 1)
                dve.wait_ge(exped, b + 1)
                link(nc.vector.tensor_reduce(small[:, :], gt[0:HC, :, 0:HC], AX.X, ALU.add))
                link(nc.vector.reciprocal(small[:, :], small[:, :]))
                nc.vector.tensor_tensor(attn[:, :, :], gt[0:HC, :, 0:HC], over(small), ALU.mult).then_inc(attn_made, 1)
                dve.wait_ge(mt_ps, b + 1)
                for g in range(2):
                    link(nc.vector.tensor_tensor(mt[:, 2 * g:2 * g + 2, :],
                                                 misc[g][0:HC, 0:2 * C].rearrange("p (h c) -> p h c", h=2),
                                                 r0up[0:HC, :].rearrange("p (a c) -> p a c", a=1).to_broadcast([HC, 2, C]),
                                                 ALU.mult))

                def fold(t):
                    n = b * TAPS + t
                    if t >= 2:
                        dve.wait_ge(e_ps, n - 1)
                    nc.vector.tensor_tensor(dm[:, t % 2, :, :], mt[:, :, :],
                                            wdv[:, :, t:t + 1].to_broadcast([HC, HEADS, C]), ALU.mult).then_inc(dm_made, 1)

                fold(0)
                for t in range(TAPS):
                    n = b * TAPS + t
                    if t + 1 < TAPS:
                        fold(t + 1)
                    dve.wait_ge(e_ps, n + 1)
                    dve.wait_ge(e_lo, 1 + n)
                    src = misc[t % 2][:, 0:2 * C].rearrange("p (i c) -> p i c", i=2)
                    if t == TAPS // 2:
                        nc.vector.tensor_tensor(esum[:, :, :], src, res_eye[:, :, :], ALU.add).then_inc(e_sum, 1)
                    else:
                        nc.vector.tensor_copy(esum[:, :, :], src).then_inc(e_sum, 1)
                    dve.wait_ge(e_hi, n + 1)
                    nc.vector.tensor_tensor(e_v[:, 1, :, t, :], esum[:, :, :], e_v[:, 0, :, t, :], ALU.subtract)\
                        .then_inc(e_lo, 1)

            def z_final(b, ahead):
                dve.wait_ge(zsum_ps, 1 + b + 1)
                dve.wait_ge(sd_made, b * 2 + 2 if ahead else b * 2 + 1)
                for i, t in enumerate((st_m, st_v)):
                    link(nc.vector.tensor_reduce(t[:, 0:GROUPS],
                                                 misc[i][:, 0:2 * C].rearrange("p (r g c) -> p g r c", r=2, c=GC),
                                                 AX.XY, ALU.add))
                dve.sem_inc(zsum_read, 1)
                link(nc.vector.tensor_scalar(st_v[:, 0:GROUPS], st_v[:, 0:GROUPS], 1.0 / N_GROUP, None, ALU.mult))
                link(nc.vector.tensor_scalar(st_m[:, 0:GROUPS], st_m[:, 0:GROUPS], 1.0 / N_GROUP, None, ALU.mult))
                sd0 = t_sd[:, bass.ds(b, 1), :].rearrange("p a g -> p (a g)")
                link(nc.vector.tensor_tensor(st_t[:, 0:GROUPS], st_m[:, 0:GROUPS], st_m[:, 0:GROUPS], ALU.mult))
                link(nc.vector.tensor_tensor(st_v[:, 0:GROUPS], st_v[:, 0:GROUPS], st_t[:, 0:GROUPS], ALU.subtract))
                link(nc.vector.tensor_tensor(st_v[:, 0:GROUPS], st_v[:, 0:GROUPS], sd0, ALU.mult))
                link(nc.vector.tensor_tensor(st_v[:, 0:GROUPS], st_v[:, 0:GROUPS], sd0, ALU.mult))
                nc.vector.tensor_scalar(st_v[:, 0:GROUPS], st_v[:, 0:GROUPS], 0.0, EPS, ALU.max, ALU.add).then_inc(var_made, 1)
                dve.wait_ge(sd_made, b * 2 + 3 if ahead else b * 2 + 2)
                link(nc.vector.reciprocal(st_v[:, 0:GROUPS], st_t[:, 0:GROUPS]))
                s1 = t_s1[:, bass.ds(b, 1), :].rearrange("p a g -> p (a g)")
                link(nc.vector.tensor_tensor(s1, st_v[:, 0:GROUPS], sd0, ALU.mult))
                link(nc.vector.tensor_tensor(t_s1m[:, bass.ds(b, 1), :].rearrange("p a g -> p (a g)"), s1,
                                             st_m[:, 0:GROUPS], ALU.mult))

            def image(b, ahead):
                def tiles(it, n_stats):
                    done = 0
                    for s in range(2):
                        k = b * TILES + it * 2 + s
                        for q in range(BANKS_T):
                            dve.wait_ge(qk_hi, k * BANKS_T + q + 1)
                            nc.vector.tensor_tensor(tile_out(q, 1), tile_in(s, q), tile_out(q, 0), ALU.subtract)\
                                .then_inc(qk_split, 1)
                            if ahead and (s * BANKS_T + q) % 4 == 3 and done < n_stats:
                                slot = S_SLOTS[done]
                                per, before = S_SLOTS.count(slot), S_SLOTS[:done].count(slot)
                                stats_load(slot, first_loads(slot, b, 0, it * per + before + 1), it * S_ITER + done)
                                done += 1

                with dve.Fori(0, TILES // 2 - 1) as it:
                    tiles(it, S_ITER)
                tiles(TILES // 2 - 1, 2)
                attention(b)
                if ahead:
                    stats_final(b + 1, b * 2 + 2)

                def z_lo(j, r):
                    pair = b * (H // 2) + j * PAIRS + r
                    dve.wait_ge(z_copied, 4 + pair + 1)
                    for i in range(2):
                        last = nc.vector.tensor_tensor(z_out[:, :, 2 * r + i, 1, :],
                                                       zf[:, r % 2, i * C:(i + 1) * C].rearrange("p (g c) -> p g c", c=CG),
                                                       z_out[:, :, 2 * r + i, 0, :], ALU.subtract)
                    last.then_inc(z_split, 1)

                for r in range(PAIRS):
                    z_lo(0, r)
                with dve.Fori(1, CHUNKS) as j:
                    for r in range(PAIRS):
                        z_lo(j, r)
                        if ahead and r < 2:
                            normalise_scale(b + 1, j - 1, r, b)
                        if ahead and r >= 1 and r < 3:
                            normalise_lo(b + 1, j - 1, r - 1)
                    if ahead:
                        y_low(b + 1, j - 1)
                if ahead:
                    for slot in range(2):
                        normalise_scale(b + 1, CHUNKS - 1, slot, b)
                    for slot in range(2):
                        normalise_lo(b + 1, CHUNKS - 1, slot)
                    y_low(b + 1, CHUNKS - 1)
                z_final(b, ahead)

            with dve.Fori(0, CHUNKS) as j:
                for slot in range(2):
                    stats_load(slot, first_loads(slot, None, 0, j + 1), j * 2 + slot)
            stats_final(0, 1)
            with dve.Fori(0, CHUNKS) as j:
                for slot in range(2):
                    normalise_scale(0, j, slot)
                    normalise_lo(0, j, slot)
                y_low(0, j)
            base = chain[1]
            with dve.Fori(0, B - 1) as b:
                chain[1] = 0
                chain[0] = b * LINKS + base
                image(b, True)
                assert chain[1] == LINKS, chain[1]
            chain[0] = (B - 1) * LINKS + base
            chain[1] = 0
            image(B - 1, False)

        layer0_block.close()
        layer0.close()
        stack.pop()
        layer1 = ctx.enter_context(ExitStack())
        stack.append(layer1)
        wide = sb("wide", [P, 2, CG, 2, W], f16)
        zin = sb("zin", [P, 2, H, 2, CG], f16)
        mixed_out = sb("mixed_out", [P, 2, CG, W])
        shift = sb("shift", [P, B, C])
        wsum = sb("wsum", [P, C])
        wsum_in = sb("wsum_in", [PIECES, C])
        bias_row = sb("bias_row", [P, C])
        held = sb("held", [PIECES, P])

        b_in = sem("b_in")
        held_made = sem("held_made")
        wsum_ps = sem("wsum_ps")
        shift_step = sem("shift_step")
        wide_in = [sem("wide_in0"), sem("wide_in1")]
        z_in = [sem("z_in0"), sem("z_in1")]
        quad_full = sem("quad_full")
        shifted = sem("shifted")
        quad_out = sem("quad_out")
        stored = sem("stored")
        out_free = sem("out_free")

        block1 = ctx.enter_context(nc.Block())

        @block1.sync
        def _(sp):
            sp.dma_start(wsum_in[:, :], wide_t).then_inc(b_in, 16)
            sp.dma_start(bias_row[:, :], bias.rearrange("(a c) -> a c", a=1).to_broadcast([P, C])).then_inc(b_in, 16)
            sp.wait_ge(held_made, 1)
            for g in range(CGROUPS):
                if g >= 2:
                    sp.wait_ge(quad_full, 2 * QUADS + (g - 1) * B * QUADS)
                sp.dma_start(wide[:, g % 2, :, :, :],
                             bass.AP(tensor=tab_dram.tensor, offset=g * CG * 4 * W + 1,
                                     ap=[[1, P], [4 * W, CG], [2 * W, 2], [1, W]])).then_inc(wide_in[g % 2], 16)
                with sp.Fori(0, B // 2) as i:
                    for s in range(2):
                        sp.wait_ge(quad_full, (g * B + i * 2 + s) * QUADS + QUADS)
                        sp.dma_start(zin[:, s, :, :, :].rearrange("p h s c -> p (h s c)"),
                                     z_dram[bass.ds(i * 2 + s, 1), :, g, :, :, :]
                                     .rearrange("b p h s c -> p (b h s c)")).then_inc(z_in[s], 16)

        @block1.gpsimd
        def _(pool):
            nc.gpsimd.memset(held[:, :], float(PIECE)).then_inc(held_made, 1)
            with pool.Fori(0, CGROUPS) as g:
                with pool.Fori(0, B // 2) as i:
                    for s in range(2):
                        pool.wait_ge(quad_out, 3 + (g * B + i * 2 + s) * QUADS + QUADS)
                        pool.dma_start(out[bass.ds(i * 2 + s, 1), bass.ds(g * CG, CG), :, :].rearrange("b c h w -> h (b c) w"),
                                       mixed_out[:, s, :, :]).then_inc(stored, 16)
                        pool.wait_ge(stored, (g * B + i * 2 + s + 1) * 16)
                        pool.sem_inc(out_free, 1)
            pool.wait_ge(stored, 16 * CGROUPS * B)

        @block1.tensor
        def _(pe):
            pe.sem_inc(quad_full, 2 * QUADS)
            pe.wait_ge(b_in, 32)
            pe.wait_ge(held_made, 1)
            nc.tensor.matmul(psum[7][:, 0:C], held[:, :], wsum_in[:, :], start=True, stop=True).then_inc(wsum_ps, 1)
            with pe.Fori(0, CGROUPS // 2) as gp:
                for gs_ in range(2):
                    pe.wait_ge(wide_in[gs_], (gp + 1) * 16)
                    pe.sem_inc(carried, 1)
                    with pe.Fori(0, B // 2) as i:
                        for s in range(2):
                            step = gp * (2 * B) + gs_ * B + i * 2 + s
                            pe.wait_ge(z_in[s], (gp * B + gs_ * (B // 2) + i + 1) * 16)
                            for q in range(QUADS):
                                pe.wait_ge(quad_out, step * QUADS + q + 1)
                                for k in range(QUAD):
                                    c = q * QUAD + k
                                    z_hi, z_lo = zin[:, s, :, 0, c], zin[:, s, :, 1, c]
                                    w_hi, w_lo = wide[:, gs_, c, 0, ::-1], wide[:, gs_, c, 1, ::-1]
                                    conv = psum[q % 3][:, k * W:(k + 1) * W]
                                    res = psum[3 + q % 3][:, k * W:(k + 1) * W]
                                    nc.tensor.matmul(conv, z_hi, w_hi, start=True, stop=False, skip_group_check=True)
                                    nc.tensor.matmul(conv, z_hi, w_lo, start=False, stop=False, skip_group_check=True)
                                    nc.tensor.matmul(res, z_hi, ident16[:, :], start=True, stop=False, skip_group_check=True)
                                    nc.tensor.matmul(conv, z_lo, w_hi, start=False, stop=True, skip_group_check=True)
                                    last = nc.tensor.matmul(res, z_lo, ident16[:, :], start=False, stop=True,
                                                            skip_group_check=True)
                                last.then_inc(quad_full, 1)

        @block1.scalar
        def _(act):
            act.wait_ge(shift_step, 1 + 3 * B)
            with act.Fori(0, CGROUPS) as g:
                with act.Fori(0, B // 2) as i:
                    for s in range(2):
                        step = g * B + i * 2 + s
                        act.wait_ge(out_free, step + 1)
                        sd = t_sd[:, bass.ds(i * 2 + s, 1), :].rearrange("p a g -> p (a g)")[:, bass.ds(g * (CG // GC), CG // GC)]
                        sh = shift[:, bass.ds(i * 2 + s, 1), :].rearrange("p a c -> p (a c)")[:, bass.ds(g * CG, CG)]
                        for q in range(QUADS):
                            act.wait_ge(quad_full, step * QUADS + 2 * QUADS + q + 1)
                            for k in range(QUAD):
                                c = q * QUAD + k
                                last = nc.scalar.activation(mixed_out[:, s, c, :], psum[3 + q % 3][:, k * W:(k + 1) * W],
                                                            ACT.Identity, scale=sd[:, c // GC:c // GC + 1],
                                                            bias=sh[:, c:c + 1])
                            last.then_inc(shifted, 1)

        @block1.vector
        def _(dve):
            dve.sem_inc(quad_out, 3)
            dve.sem_inc(out_free, 2)
            dve.wait_ge(wsum_ps, 1)
            nc.vector.tensor_copy(wsum[:, :], psum[7][:, 0:C]).then_inc(shift_step, 1)
            for b in range(B):
                def wide_row(t):
                    return t[:, b, :].rearrange("p (g a) -> p g a", a=1).to_broadcast([P, GROUPS, GC])

                row = shift[:, b, :].rearrange("p (g c) -> p g c", c=GC)
                dve.wait_ge(shift_step, 1 + 3 * b)
                nc.vector.tensor_tensor(row, wsum[:, :].rearrange("p (g c) -> p g c", c=GC), wide_row(t_s1m), ALU.mult)\
                    .then_inc(shift_step, 1)
                dve.wait_ge(shift_step, 2 + 3 * b)
                nc.vector.tensor_tensor(row, wide_row(t_mean), row, ALU.subtract).then_inc(shift_step, 1)
                dve.wait_ge(shift_step, 3 + 3 * b)
                nc.vector.tensor_tensor(shift[:, b, :], shift[:, b, :], bias_row[:, :], ALU.add).then_inc(shift_step, 1)
            with dve.Fori(0, CGROUPS) as g:
                with dve.Fori(0, B // 2) as i:
                    for s in range(2):
                        step = g * B + i * 2 + s
                        sc = t_s1[:, bass.ds(i * 2 + s, 1), :].rearrange("p a g -> p (a g)")[:, bass.ds(g * (CG // GC), CG // GC)]
                        for q in range(QUADS):
                            dve.wait_ge(shifted, step * QUADS + q + 1)
                            for k in range(QUAD):
                                c = q * QUAD + k
                                last = nc.vector.scalar_tensor_tensor(mixed_out[:, s, c, :], psum[q % 3][:, k * W:(k + 1) * W],
                                                                      sc[:, c // GC:c // GC + 1], mixed_out[:, s, c, :],
                                                                      ALU.mult, ALU.add)
                            last.then_inc(quad_out, 1)


def kernel(**inputs):
    import numpy as np
    import concourse.bacc as bacc
    from concourse import mybir
    from concourse.bass_utils import run_bass_kernel_spmd

    a = {k: np.asarray(v) for k, v in inputs.items()}
    order = np.concatenate([np.concatenate([np.arange(h * HC, (h + 1) * HC), C + np.arange(h * HC, (h + 1) * HC)])
                            for h in range(HEADS)])
    w_qkv, w_dw = a["L0_conv_w_qkv"], a["L0_conv_w_dw"].reshape(3 * C, TAPS)
    wide = a["L1_conv_weights"].reshape(C, PIECES)
    ch = np.arange(C)
    same = (ch[:, None] // GC == ch[None, :] // GC).astype(np.float32)
    cols = np.concatenate([ch[:CA], ch[CA:], ch[CA:]])
    p, n, d = np.arange(P)[:, None, None], np.arange(BAND)[None, None, :], np.arange(3)[None, :, None]
    masks = ((p % TC == n % TC) & (p // TC - n // TC == d)).astype(np.float32)
    arrays = {
        "x": a["x"],
        "w_qk": w_qkv[order].T, "w_v": w_qkv[2 * C:][:, cols].reshape(HEADS, HC, 2 * P).transpose(1, 0, 2).reshape(HC, -1),
        "w_dw_qk": w_dw[order].reshape(TC, TG * TAPS), "masks": masks, "w_dw_v": w_dw[2 * C:],
        "w_proj_t": a["L0_conv_w_proj"].T, "temperature": a["L0_conv_temperature"].reshape(HEADS),
        "wide_w": wide, "wide_t": wide.T, "bias": a["L1_conv_bias"],
        "group_a": same[:CA][:, cols] / np.float32(GC),
        "group_b": np.concatenate([same[CA:], np.zeros_like(same[CA:])])[:, cols] / np.float32(GC),
        "ident": np.eye(P, dtype=np.float32),
        "res_eye": np.float32(UP) * np.stack([np.eye(C, dtype=np.float32)[:CA],
                                              np.eye(C, dtype=np.float32)[np.concatenate([ch[CA:], ch[CA:]])]], axis=1),
    }
    nc = bacc.Bacc("TRN2", target_bir_lowering=False, num_devices=1)
    arrays = {f"in_{k}": np.ascontiguousarray(v) for k, v in arrays.items()}
    args = [nc.dram_tensor(k, v.shape, mybir.dt.from_np(v.dtype), kind="ExternalInput").ap() for k, v in arrays.items()]
    out = nc.dram_tensor("out", [B, C, H, W], mybir.dt.float32, kind="ExternalOutput").ap()
    conv_kernel(nc, *args, out)
    result = run_bass_kernel_spmd(nc, [arrays], core_ids=[0])
    return result.results[0]["out"]
```

```python
import concourse.bass as bass
from concourse import mybir
from contextlib import ExitStack

B, C, H, W = 8, 192, 128, 128
HEADS, HC = 4, 48
GROUPS, GC = 32, 6
TAPS = 9
PIECES, PIECE = 16, 8
EPS = 1e-5
NORM_EPS = 1e-12

P = 128
CA = 128
CB = C - CA
QK = 2 * C
HQK = 2 * HC
UP = 64.0
N_GROUP = GC * H * W
LOAD_ROWS = 4
LOADS = H // LOAD_ROWS
NLOAD = LOAD_ROWS * W
TR, TC, TG = 8, 16, 24
TOUT = TR - 2
BAND = TC * TOUT
TILES = -(-H // TOUT)
WP = W + 2
Y_ROWS = (TILES - 1) * TOUT + TR
GV = C // TC
GPB = 4
BANKS_T, BANKS_V = TG // GPB, GV // GPB
GVA = CA // TC
ITERS = TILES // 2
PAIRS_T = TOUT // 2
BLOCKS = [(t * P, (t + 1) * P) for t in range(QK // P)] + [(QK, QK + CA), (QK + CA, QK + C)]
NB = len(BLOCKS)
SLOTS = (0, 1, 0)
PER = len(SLOTS)
LAST_LOADS = LOADS - (ITERS - 1) * PER
IN_SLOT = [SLOTS.count(s) * (ITERS - 1) + 1 for s in range(2)]
AHEAD = 2
BEFORE_PAIR = [range(0, 3), range(3, 4), range(4, NB)]
FIRST_ROWS = 2 * LOAD_ROWS
FIRST_SLOTS = H * W * 2 // (2 * FIRST_ROWS * W * 4)
CG = 24
CGROUPS = C // CG
QUAD = 4
QUADS = CG // QUAD


def conv_kernel(nc, x, w_qk, w_dw, masks_in, select_in, w_proj_t, temperature, wide_w, wide_t, bias,
                group_a, group_b, ident_in, res_eye_in, out):
    f32, f16 = mybir.dt.float32, mybir.dt.float16
    ALU = mybir.AluOpType
    ACT = mybir.ActivationFunctionType
    AX = mybir.AxisListType

    ctx = ExitStack()
    with ctx:
        def sb(name, shape, dt=f32):
            return stack[-1].enter_context(nc.sbuf_tensor(name, shape, dt))

        def sem(name):
            return ctx.enter_context(nc.semaphore(name))

        stack = [ctx]
        z_dram = nc.dram_tensor("z_scratch", [B, P, CGROUPS, H, 2, CG], f16).ap()
        yv_dram = nc.dram_tensor("yv_scratch", [B, Y_ROWS, C, 2, WP], f16).ap()
        y_dram = nc.dram_tensor("y_scratch", [Y_ROWS, QK, 2, WP], f16).ap()
        tab_dram = nc.dram_tensor("wide_table", [C, 2, 2 * W], f16).ap()

        t_mean = sb("t_mean", [P, B, GROUPS])
        t_sd = sb("t_sd", [P, B, GROUPS])
        t_s1 = sb("t_s1", [P, B, GROUPS])
        t_s1m = sb("t_s1m", [P, B, GROUPS])
        ident = sb("ident", [P, P])
        ident16 = sb("ident16", [P, P], f16)
        ones = sb("ones", [P, P])

        psum = [ctx.enter_context(nc.psum_tensor(f"bank{i}", [P, 512], f32)) for i in range(8)]
        acc, gram, misc = psum[0:4], psum[4:6], psum[6:8]

        layer0 = ExitStack()
        layer0_block = ExitStack()
        stack.append(layer0)
        xa_hi = sb("xa_hi", [P, H, W], f16)
        xa_lo = sb("xa_lo", [P, H, W], f16)
        xb = sb("xb", [P, H, W], f16)
        w1 = sb("w1", [P, 2, 2, 3 * C], f16)
        bands = sb("bands", [P, 2, TG + GV, 3, BAND], f16)
        m16 = sb("m16", [P, 2, 2, C], f16)
        eye16 = sb("eye16", [P, 2, C], f16)
        rows_sp = sb("rows_sp", [P, TOUT * 2 * QK], f16)
        qk = rows_sp[:, :].rearrange("p (r s c) -> p r s c", r=TOUT, s=2)
        vrow = rows_sp[:, 0:TOUT * QK].rearrange("p (r c) -> p r c", r=TOUT)
        vt = rows_sp[:, TOUT * QK:].rearrange("p (r c) -> p r c", r=TOUT)
        stage = sb("stage", [P, 2, 2, NLOAD])
        sq = sb("sq", [P, 2 * C])
        stage_hi = sb("stage_hi", [P, NLOAD], f16)
        zeros = sb("zeros", [P, P], f16)
        space = sb("space", [P, 8792])

        def view(at, parts, shape, dt=f32):
            size = 4 if dt == f32 else 2
            n = 1
            for k in shape:
                n *= k
            v = space[0:parts, at // 4:(at + n * size) // 4]
            if dt != f32:
                v = v.bitcast(dt)
            names = " ".join(f"d{i}" for i in range(len(shape)))
            return v.rearrange(f"p ({names}) -> p {names}", **{f"d{i}": k for i, k in enumerate(shape)})

        y2 = [view(at, P, [TG, 2, WP], f16) for at in (22688, 0)]
        gs = view(0, HQK, [HEADS, 2 * HQK])
        gg = view(3072, HQK, [HEADS, HQK])
        gt = view(4608, HQK, [HEADS, HQK])
        kn = view(6144, HC, [HEADS, HC])
        attn = view(6912, HC, [HEADS, HC])
        mt = view(7680, HC, [HEADS, C])
        wpt = view(10752, HC, [HEADS, C])
        select = view(18432, HC, [HEADS, 2, P])
        colb = view(0, P, [2, 2, P])
        z_out = view(0, P, [CGROUPS, TOUT, 2, CG], f16)
        zf = view(4608, P, [PAIRS_T, 2 * C])
        sum_z = view(9216, P, [2 * C])
        sum_q = view(10752, P, [2 * C])
        ystage = view(12288, P, [NB, LOAD_ROWS, 2, WP], f16)
        y2v = [view(22688 + s * GV * 2 * WP * 2, P, [GV, 2, WP], f16) for s in range(2)]
        table = view(12288, HQK, [2, 2, 2 * W], f16)
        wide_tmp = view(16384, HQK, [2, PIECES])
        eye_tmp = view(17408, P, [2, C])
        wv_tmp = view(26112, P, [2, C])
        wcol = view(27648, P, [TG + GV, TAPS])
        masks = view(28944, P, [3, BAND])
        band_sum = rows_sp[:, :].bitcast(f32).rearrange("p (g n) -> p g n", n=BAND)
        band_tmp = view(3072, P, [TG, BAND])
        first_rows = xa_lo[:, :, :].rearrange("p h w -> p (h w)").bitcast(f32)\
            .rearrange("p (s k n) -> p s k n", s=FIRST_SLOTS, k=2)
        grp_a = sb("grp_a", [P, 2 * P])
        grp_b = sb("grp_b", [P, 2 * P])
        temp = sb("temp", [HC, HEADS])
        stats = sb("stats", [P, 2, LOADS, 6])
        mv = sb("mv", [P, 2, 2])
        col = sb("col", [P, 2, 2])
        st_m = sb("st_m", [P, GROUPS + 2])
        st_v = sb("st_v", [P, GROUPS + 2])
        st_t = sb("st_t", [P, GROUPS + 2])
        nbias = sb("nbias", [P, 2])
        st_scale = sb("st_scale", [P, 2])
        r0up = sb("r0up", [P, C])
        small = sb("small", [HC, HEADS])
        qn = sb("qn", [HC, HEADS])

        first_loaded = [sem(f"first_loaded{slot}") for slot in range(FIRST_SLOTS)]
        carried = sem("carried")
        const_loaded = sem("const_loaded")
        loaded = [sem("loaded0"), sem("loaded1")]
        stats_used = sem("stats_used")
        w1_made = sem("w1_made")
        band_step = sem("band_step")
        bands_made = sem("bands_made")
        y_zeroed = sem("y_zeroed")
        borders = sem("borders")
        y_full = sem("y_full")
        y_hi = sem("y_hi")
        y_split = sem("y_split")
        y_stored = [sem(f"y_stored{t}") for t in range(NB)]
        v_loaded = [sem("v_loaded0"), sem("v_loaded1")]
        v_full = sem("v_full")
        v_hi = sem("v_hi")
        v_split = sem("v_split")
        t_full = sem("t_full")
        t_copied = sem("t_copied")
        m_full = sem("m_full")
        m_hi = sem("m_hi")
        m_split = sem("m_split")
        y2_loaded = [sem("y2_loaded0"), sem("y2_loaded1")]
        tile_full = sem("tile_full")
        attn_loaded = sem("attn_loaded")
        pads_zero = sem("pads_zero")
        taps_in = sem("taps_in")
        consts_made = sem("consts_made")
        table_made = sem("table_made")
        table_stored = sem("table_stored")
        affine = sem("affine")
        hi_made = sem("hi_made")
        normed = sem("normed")
        acc_full = sem("acc_full")
        qk_hi = sem("qk_hi")
        qk_split = sem("qk_split")
        gram_tiles = sem("gram_tiles")
        z_copied = sem("z_copied")
        z_split = sem("z_split")
        z_summed = sem("z_summed")
        z_stored = sem("z_stored")
        sums_zero = sem("sums_zero")
        pool_step = sem("pool_step")
        zsum_ps = sem("zsum_ps")
        zsum_read = sem("zsum_read")
        st_read = sem("st_read")
        step_v = sem("step_v")
        st_col = sem("st_col")
        st_ps = sem("st_ps")
        var_made = sem("var_made")
        sd_made = sem("sd_made")
        gram_copied = sem("gram_copied")
        gram_closed = sem("gram_closed")
        gram_t = sem("gram_t")
        diag_made = sem("diag_made")
        colsum = sem("colsum")
        norms_ready = sem("norms_ready")
        norms_rooted = sem("norms_rooted")
        logits = sem("logits")
        exped = sem("exped")
        attn_made = sem("attn_made")
        mt_ps = sem("mt_ps")
        mt_made = sem("mt_made")

        def settled(engine):
            engine.sem_inc(carried, 1)

        def quad_rows(i, n):
            return (xa_hi, xa_lo, xb)[i][:, bass.ds(n * LOAD_ROWS, LOAD_ROWS), :]

        def y_bank(i, t):
            return (gram[0], gram[1], misc[1])[(i * NB + t) % 3]

        def unit(b, it, i, t):
            return (b * LOADS + it * PER + i) * NB + t

        def tile_in(s, q):
            return acc[(s * BANKS_T + q) % 4][:, 0:GPB * BAND].rearrange("p (g r c) -> p r c g", r=TOUT, c=TC)

        def tile_out(q, low):
            return qk[:, :, low, :].rearrange("p r (c g) -> p r c g", g=TG)[:, :, :, q * GPB:(q + 1) * GPB]

        def value_in(s, q):
            return acc[(s * BANKS_V + q) % 2][:, 0:GPB * BAND].rearrange("p (g r c) -> p r c g", r=TOUT, c=TC)

        def value_out(q, low):
            if q * GPB < GVA:
                v = vrow[:, :, low * CA:(low + 1) * CA].rearrange("p r (c g) -> p r c g", g=GVA)
                return v[:, :, :, q * GPB:(q + 1) * GPB]
            v = vrow[:, :, 2 * CA + low * CB:2 * CA + (low + 1) * CB]
            return v.rearrange("p r (c g) -> p r c g", g=GV - GVA)

        def z_bank(s, rp):
            return acc[2 + (s * PAIRS_T + rp) % 2]

        def pair_of(b, it, s, rp):
            return b * (H // 2) + (it * 2 + s) * PAIRS_T + rp

        def rows(ap):
            return ap.rearrange("p (r c) -> p r c", c=W)

        def loop(engine, body):
            body(0, True, False)
            with engine.Fori(1, ITERS - 1) as it:
                body(it, False, False)
            body(ITERS - 1, False, True)

        def pairs_in(s, last):
            return (H - (TILES - 1) * TOUT) // 2 if last and s else PAIRS_T

        PRODUCTS = [(0, 0, 0), (0, 1, 0), (1, 0, 0), (2, 0, 1), (2, 1, 1)]
        N_CONST = 14
        BELOW = Y_ROWS - H - 1
        ZERO_IN = -(-BELOW * QK * 2 * WP // (P * W))
        ZERO_STORES = 2 * (B + 1)

        block = layer0_block.enter_context(nc.Block())

        @block.sync
        def _(sp):
            for dst, src in (
                (grp_a[:, :], group_a), (grp_b[:, :], group_b), (ident[:, :], ident_in),
                (eye_tmp, res_eye_in),
                (temp[:, :], temperature.rearrange("(a h) -> a h", a=1).to_broadcast([HC, HEADS])),
                (stage[:, 1, 0, 0:QK], w_qk[0:CA, 0:QK]),
                (stage[0:CB, 1, 1, 0:QK], w_qk[CA:C, 0:QK]),
                (stage[CB:P, 1, 1, 0:QK], w_qk[CA:C, 0:QK]),
                (wv_tmp[:, 0, :], w_qk[0:CA, QK:3 * C]),
                (wv_tmp[0:CB, 1, :], w_qk[CA:C, QK:3 * C]),
                (wv_tmp[CB:P, 1, :], w_qk[CA:C, QK:3 * C]),
                (masks, masks_in),
                (wide_tmp[:, 0, :], wide_w[0:HQK, :]), (wide_tmp[:, 1, :], wide_w[HQK:C, :]),
            ):
                sp.dma_start(dst, src).then_inc(const_loaded, 16)
            for r in range(TR):
                sp.dma_start(wcol[r * TC:(r + 1) * TC].rearrange("p g t -> p (g t)"), w_dw).then_inc(taps_in, 16)
            sp.wait_ge(pads_zero, 1)
            zero_px = xa_hi[:, 0:ZERO_IN, :].rearrange("p r w -> p (r w)")

            def store_zeros(dst):
                dst = dst.rearrange("r c s w -> (r c s w)").rearrange("(p n) -> p n", p=P)
                sp.dma_start(dst, zero_px[:, 0:dst.shape[1]]).then_inc(y_zeroed, 16)

            store_zeros(y_dram[0:1, :, :, :])
            store_zeros(y_dram[H + 1:Y_ROWS, :, :, :])
            for b in range(B):
                store_zeros(yv_dram[b, 0:1, :, :, :])
                store_zeros(yv_dram[b, H + 1:Y_ROWS, :, :, :])
            sp.wait_ge(table_made, 2)
            for part in range(2):
                sp.dma_start(tab_dram[part * HQK:(part + 1) * HQK, :, :], table[:, part, :, :]).then_inc(table_stored, 16)

            def load_first(j, slot):
                row = (j * FIRST_SLOTS + slot) * FIRST_ROWS
                for dst, c0, c1 in ((first_rows[:, slot, 0, :], 0, CA), (first_rows[0:CB, slot, 1, :], CA, C)):
                    sp.dma_start(dst, x[0, c0:c1, bass.ds(row, FIRST_ROWS), :].rearrange("c h w -> c (h w)"))\
                        .then_inc(first_loaded[slot], 16)

            for slot in range(FIRST_SLOTS):
                load_first(0, slot)
            with sp.Fori(1, H // (FIRST_SLOTS * FIRST_ROWS)) as j:
                for slot in range(FIRST_SLOTS):
                    sp.wait_ge(stats_used, 2 + ((j - 1) * FIRST_SLOTS + slot + 1) * (FIRST_ROWS // LOAD_ROWS))
                    settled(sp)
                    load_first(j, slot)
            sp.wait_ge(w1_made, 1)

            def load(b, it, i, blocks):
                slot = SLOTS[i]
                for dst, c0, c1 in ((stage[:, slot, 0, :], 0, CA), (stage[0:CB, slot, 1, :], CA, C),
                                    (stage[CB:P, slot, 1, :], CA, C))[0:blocks]:
                    src = x[bass.ds(b, 1), c0:c1, bass.ds((it * PER + i) * LOAD_ROWS, LOAD_ROWS), :]
                    sp.dma_start(dst, src.rearrange("b c h w -> c (b h w)")).then_inc(loaded[slot], 16)

            def load_for_stats(b, it, i):
                sp.wait_ge(stats_used, b * LOADS + it * PER + i + (1 if i == 2 else 2))
                settled(sp)
                load(b, it, i, 2)

            def load_to_normalise(b, it, i):
                sp.wait_ge(normed, b * LOADS + it * PER + i + (2, 0, 1)[i])
                settled(sp)
                load(b, it, i, 3)

            def store_y(b, it, i):
                first_row = (it * PER + i) * LOAD_ROWS + 1
                for t, (c0, c1) in enumerate(BLOCKS):
                    sp.wait_ge(y_split, 3 + unit(b, it, i, t) + 1)
                    if c0 < QK:
                        dst = y_dram[bass.ds(first_row, LOAD_ROWS), c0:c1, :, :].rearrange("r p s w -> p r (s w)")
                    else:
                        dst = yv_dram[bass.ds(b, 1), bass.ds(first_row, LOAD_ROWS), c0 - QK:c1 - QK, :, :]\
                            .rearrange("b r p s w -> p (b r) (s w)")
                    sp.dma_start(dst, ystage[0:c1 - c0, t, :, :, :].rearrange("p r s w -> p r (s w)")).then_inc(y_stored[t], 16)

            def load_tile(b, it, s):
                k = it * 2 + s
                sp.wait_ge(tile_full, (b * TILES + k + 1) * BANKS_T)
                sp.dma_start(y2[s].rearrange("p g s w -> p (g s w)"),
                             y_dram[bass.ds(k * TOUT, TR), :, :, :].rearrange("r (c g) s w -> (r c) (g s w)", c=TC))\
                    .then_inc(y2_loaded[s], 16)

            def load_values(b, it, s):
                k = it * 2 + s
                sp.wait_ge(v_full, (b * TILES + k + 1) * BANKS_V)
                sp.dma_start(y2v[s].rearrange("p g s w -> p (g s w)"),
                             yv_dram[bass.ds(b, 1), bass.ds(k * TOUT, TR), :, :, :]
                             .rearrange("b r (c g) s w -> (b r c) (g s w)", c=TC)).then_inc(v_loaded[s], 16)

            def store_z(b, it, s, n_pairs):
                sp.wait_ge(z_split, PAIRS_T + pair_of(b, it, s, n_pairs - 1) + 1)
                sp.dma_start(z_dram[bass.ds(b, 1), :, :, bass.ds((it * 2 + s) * TOUT, 2 * n_pairs), :, :]
                             .rearrange("b p g r s c -> p (b g) (r s c)"),
                             z_out[:, :, 0:2 * n_pairs, :, :].rearrange("p g r s c -> p g (r s c)")).then_inc(z_stored, 16)

            def load_first_tile(b):
                sp.wait_ge(v_full, 2 * BANKS_V + b * TILES * BANKS_V)
                settled(sp)
                for t in range(QK // P):
                    sp.wait_ge(y_stored[t], 16 + (b * LOADS + 2) * 16)
                    settled(sp)
                load_tile(b, 0, 0)

            def image(b, ahead):
                sp.wait_ge(zsum_ps, 1 + b)
                sp.wait_ge(z_stored, 16 + b * TILES * 16)
                for t in range(NB):
                    sp.wait_ge(y_stored[t], 16 + (b + 1) * LOADS * 16)
                    settled(sp)
                sp.wait_ge(normed, 2 + (b + 1) * LOADS)
                settled(sp)
                load_tile(b, 0, 1)
                if ahead:
                    for i in range(PER):
                        load_for_stats(b + 1, 0, i)
                with sp.Fori(1, ITERS - 1) as it:
                    for s in range(2):
                        load_tile(b, it, s)
                    if ahead:
                        for i in range(PER):
                            load_for_stats(b + 1, it, i)
                for s in range(2):
                    load_tile(b, ITERS - 1, s)
                if ahead:
                    for i in range(LAST_LOADS):
                        load_for_stats(b + 1, ITERS - 1, i)
                sp.wait_ge(gram_closed, b + 1)
                sp.dma_start(select.rearrange("p h i m -> p (h i m)"), select_in).then_inc(attn_loaded, 16)
                sp.dma_start(wpt, w_proj_t.rearrange("(h p) o -> p h o", p=HC)).then_inc(attn_loaded, 16)
                for s in range(2):
                    load_values(b, 0, s)
                if ahead:
                    sp.wait_ge(stats_used, 2 + (b + 2) * LOADS)
                    settled(sp)
                    load_to_normalise(b + 1, 0, 0)
                    load_to_normalise(b + 1, 0, 1)

                def body(it, first, last):
                    norm = ahead and not first
                    if norm:
                        load_to_normalise(b + 1, it - 1, 2)
                    if not last:
                        load_values(b, it + 1, 0)
                    if norm:
                        store_y(b + 1, it - 1, 0)
                    if not last:
                        load_values(b, it + 1, 1)
                    if norm:
                        load_to_normalise(b + 1, it, 1)
                        store_y(b + 1, it - 1, 1)
                        load_to_normalise(b + 1, it, 0)
                    store_z(b, it, 0, PAIRS_T)
                    if norm:
                        store_y(b + 1, it - 1, 2)
                    store_z(b, it, 1, pairs_in(1, last))

                loop(sp, body)
                if ahead:
                    load_first_tile(b + 1)
                    for i in range(LAST_LOADS):
                        store_y(b + 1, ITERS - 1, i)

            load_to_normalise(0, 0, 0)
            load_to_normalise(0, 0, 1)
            with sp.Fori(0, ITERS - 1) as it:
                load_to_normalise(0, it, 2)
                store_y(0, it, 0)
                load_to_normalise(0, it + 1, 1)
                load_to_normalise(0, it + 1, 0)
                store_y(0, it, 1)
                store_y(0, it, 2)
            sp.wait_ge(y_zeroed, 16 * ZERO_STORES)
            sp.wait_ge(bands_made, 1)
            load_first_tile(0)
            for i in range(LAST_LOADS):
                store_y(0, ITERS - 1, i)
            with sp.Fori(0, B - 1) as b:
                image(b, True)
            image(B - 1, False)
            sp.wait_ge(z_stored, 16 + 16 * B * TILES)
            sp.wait_ge(table_stored, 32)

        @block.gpsimd
        def _(pool):
            nc.gpsimd.memset(xa_hi[:, 0:ZERO_IN, :], 0.0).then_inc(pads_zero, 1)
            nc.gpsimd.memset(zeros[:, :], 0.0).then_inc(pads_zero, 1)
            nc.gpsimd.memset(ones[:, :], 1.0).then_inc(pads_zero, 1)
            def clear_borders():
                for side in (0, WP - 1):
                    nc.gpsimd.memset(ystage.rearrange("p t r s w -> p (t r s) w")[:, :, side:side + 1], 0.0)\
                        .then_inc(borders, 1)

            pool.wait_ge(const_loaded, 16 * N_CONST)
            pool.wait_ge(taps_in, 16 * TR)
            pool.wait_ge(consts_made, 1)
            pool.wait_ge(table_stored, 32)
            clear_borders()
            n = 0

            def after(ins):
                nonlocal n
                n += 1
                ins.then_inc(band_step, 1)
                pool.wait_ge(band_step, n)

            for g0, g1 in ((0, TG), (TG, TG + GV)):
                for dx in range(3):
                    total, part = band_sum[:, 0:g1 - g0], band_tmp[:, 0:g1 - g0]
                    for dy in range(3):
                        mask = masks[:, dy:dy + 1, :].to_broadcast([P, g1 - g0, BAND])
                        tap = wcol[:, g0:g1, dy * 3 + dx:dy * 3 + dx + 1].to_broadcast([P, g1 - g0, BAND])
                        after(nc.gpsimd.tensor_tensor(part if dy else total, mask, tap, ALU.mult))
                        if dy:
                            after(nc.gpsimd.tensor_tensor(total, total, part, ALU.add))
                    after(nc.gpsimd.tensor_copy(bands[:, 0, g0:g1, dx, :], total))
                    after(nc.gpsimd.tensor_tensor(bands[:, 1, g0:g1, dx, :], total, bands[:, 0, g0:g1, dx, :], ALU.subtract))
            pool.sem_inc(bands_made, 1)

            with pool.Fori(0, B) as b:
                pool.wait_ge(m_split, b + 1)
                settled(pool)
                nc.gpsimd.memset(sum_z, 0.0).then_inc(sums_zero, 1)
                nc.gpsimd.memset(sum_q, 0.0).then_inc(sums_zero, 1)
                clear_borders()
                pool.wait_ge(sums_zero, b * 2 + 2)
                settled(pool)

                def add_pair(n, slot):
                    pool.wait_ge(z_copied, 2 + n + 1)
                    pool.wait_ge(z_summed, PAIRS_T + n)
                    nc.gpsimd.tensor_tensor(sq[:, :], zf[:, slot, :], zf[:, slot, :], ALU.mult).then_inc(pool_step, 1)
                    nc.gpsimd.tensor_tensor(sum_z, sum_z, zf[:, slot, :], ALU.add).then_inc(pool_step, 1)
                    pool.wait_ge(pool_step, n * 2 + 2)
                    nc.gpsimd.tensor_tensor(sum_q, sum_q, sq[:, :], ALU.add).then_inc(z_summed, 1)

                with pool.Fori(0, H // 2 // PAIRS_T) as j:
                    for rp in range(PAIRS_T):
                        add_pair(b * (H // 2) + j * PAIRS_T + rp, rp)
                for rp in range(H // 2 % PAIRS_T):
                    add_pair(b * (H // 2) + H // 2 // PAIRS_T * PAIRS_T + rp, rp)

        @block.scalar
        def _(act):
            act.wait_ge(const_loaded, 16 * N_CONST)
            nc.scalar.activation(ident16[:, :], ident[:, :], ACT.Copy)
            nc.scalar.activation(eye16[:, :, :], eye_tmp, ACT.Copy).then_inc(consts_made, 1)

            def normalise_hi(b, it, i, parts=range(3)):
                slot, n = SLOTS[i], b * LOADS + it * PER + i
                if 0 in parts:
                    act.wait_ge(affine, n * 2 + 2)
                    nc.scalar.activation(quad_rows(0, it * PER + i), rows(stage[:, slot, 0, :]), ACT.Copy)\
                        .then_inc(hi_made, 1)
                if 1 in parts:
                    nc.scalar.activation(quad_rows(2, it * PER + i)[0:CB], rows(stage[0:CB, slot, 1, :]), ACT.Copy)\
                        .then_inc(hi_made, 1)
                if 2 in parts:
                    act.wait_ge(normed, 2 + n)
                    nc.scalar.activation(stage_hi[CB:P, :], stage[CB:P, slot, 1, :], ACT.Copy).then_inc(hi_made, 1)

            def root(n, width):
                act.wait_ge(var_made, n)
                nc.scalar.activation(st_t[:, 0:width], st_v[:, 0:width], ACT.Sqrt).then_inc(sd_made, 1)

            def y_high(b, it, i, blocks=range(NB)):
                for t in blocks:
                    m = BLOCKS[t][1] - BLOCKS[t][0]
                    act.wait_ge(y_stored[t], 16 + (b * LOADS + it * PER + i) * 16)
                    act.wait_ge(y_full, unit(b, it, i, t) + 1)
                    nc.scalar.activation(ystage[0:m, t, :, 0, 1:1 + W], rows(y_bank(i, t)[0:m, :]), ACT.Copy).then_inc(y_hi, 1)

            def step(b, it, i, it2, i2):
                for t in range(NB):
                    y_high(b, it, i, range(t, t + 1))
                    if t < 3:
                        normalise_hi(b, it2, i2, range(t, t + 1))

            def tiles(b, it):
                for s in range(2):
                    k = b * TILES + it * 2 + s
                    act.wait_ge(gram_tiles, k + 1)
                    for q in range(BANKS_T):
                        act.wait_ge(tile_full, 2 * BANKS_T + k * BANKS_T + q + 1)
                        nc.scalar.activation(tile_out(q, 0), tile_in(s, q), ACT.Copy).then_inc(qk_hi, 1)

            def value_high(b, it, s, q):
                k = b * TILES + it * 2 + s
                if q == 0:
                    act.wait_ge(t_full, 1 + k * PAIRS_T)
                act.wait_ge(v_full, 2 * BANKS_V + k * BANKS_V + q + 1)
                nc.scalar.activation(value_out(q, 0), value_in(s, q), ACT.Copy).then_inc(v_hi, 1)

            def z_pair(b, it, s, rp):
                pair = pair_of(b, it, s, rp)
                act.wait_ge(acc_full, pair + 1)
                if rp == 0:
                    act.wait_ge(z_stored, 16 + (b * TILES + it * 2 + s) * 16)
                act.wait_ge(z_split, pair + 1)
                act.wait_ge(z_summed, pair + 1)
                nc.scalar.activation(z_out[:, :, 2 * rp:2 * rp + 2, 0, :].rearrange("p g r c -> p r g c"),
                                     z_bank(s, rp)[:, 0:2 * C].rearrange("p (r g c) -> p r g c", r=2, c=CG),
                                     ACT.Copy, scale=1.0 / UP ** 2)
                nc.scalar.activation(zf[:, rp, :], z_bank(s, rp)[:, 0:2 * C], ACT.Copy,
                                     scale=1.0 / UP ** 2).then_inc(z_copied, 1)

            def attention(b):
                act.wait_ge(norms_ready, b * 2 + 2)
                nc.scalar.activation(kn, gt[0:HC, :, HC:HQK], ACT.Sqrt).then_inc(norms_rooted, 1)
                nc.scalar.activation(qn[:, :], small[:, :], ACT.Sqrt).then_inc(norms_rooted, 1)
                act.wait_ge(logits, b + 1)
                nc.scalar.activation(gt[0:HC, :, 0:HC], attn, ACT.Exp).then_inc(exped, 1)
                act.wait_ge(m_full, b + 1)
                nc.scalar.activation(m16[:, 0, :, :], misc[0][:, 0:2 * C].rearrange("p (i c) -> p i c", i=2), ACT.Copy)\
                    .then_inc(m_hi, 1)

            def image(b, ahead):
                with act.Fori(0, ITERS) as it:
                    tiles(b, it)
                attention(b)
                if ahead:
                    root(b * 2 + 2, GROUPS + 2)
                    act.wait_ge(borders, 2 * (b + 2))

                def body(it, first, last):
                    norm = ahead and not first
                    for q in range(BANKS_V):
                        value_high(b, it, 0, q)
                    if norm:
                        y_high(b + 1, it - 1, 0)
                    for q in range(BANKS_V):
                        value_high(b, it, 1, q)
                        if norm and q == 0:
                            normalise_hi(b + 1, it - 1, 1)
                    if norm:
                        for t in range(NB):
                            y_high(b + 1, it - 1, 1, range(t, t + 1))
                            if t < 3:
                                normalise_hi(b + 1, it - 1, 2, range(t, t + 1))
                    for rp in range(PAIRS_T):
                        z_pair(b, it, 0, rp)
                    if norm:
                        y_high(b + 1, it - 1, 2)
                    for rp in range(pairs_in(1, last)):
                        if ahead and rp == pairs_in(1, last) - 1:
                            normalise_hi(b + 1, it, 0)
                        z_pair(b, it, 1, rp)

                loop(act, body)
                if ahead:
                    step(b + 1, ITERS - 1, 0, ITERS - 1, 1)
                    y_high(b + 1, ITERS - 1, 1)
                root(b * 2 + 3 if ahead else b * 2 + 2, GROUPS)

            act.wait_ge(pads_zero, 3)
            act.wait_ge(y_zeroed, 16 * ZERO_STORES)
            root(1, GROUPS + 2)
            act.wait_ge(borders, 2)
            normalise_hi(0, 0, 0)
            with act.Fori(0, ITERS - 1) as it:
                for i in range(PER):
                    step(0, it, i, it + (i + 1) // PER, (i + 1) % PER)
            step(0, ITERS - 1, 0, ITERS - 1, 1)
            y_high(0, ITERS - 1, 1)
            with act.Fori(0, B - 1) as b:
                image(b, True)
            image(B - 1, False)

        @block.tensor
        def _(pe):
            def pointwise(b, it, i, blocks=range(NB)):
                pe.wait_ge(normed, 2 + b * LOADS + it * PER + i + 1)
                win = [quad_rows(j, it * PER + i) for j in range(3)]
                for t in blocks:
                    c0, c1 = BLOCKS[t]
                    pe.wait_ge(y_split, unit(b, it, i, t) + 1)
                    if c1 - c0 < P:
                        settled(pe)
                    for k, (blk, low, wblk) in enumerate(PRODUCTS):
                        last = nc.tensor.matmul(y_bank(i, t)[0:c1 - c0, :], w1[:, low, wblk, c0:c1], win[blk],
                                                start=k == 0, stop=k == len(PRODUCTS) - 1, skip_group_check=True)
                    last.then_inc(y_full, 1)

            def taps(bank, tile, g_in, g_band):
                for i in range(GPB):
                    n = 0
                    for dx in range(3):
                        for y_low, w_low in ((0, 0), (0, 1), (1, 0)):
                            last = nc.tensor.matmul(bank[:, i * BAND:(i + 1) * BAND], tile[:, g_in + i, y_low, dx:dx + W],
                                                    bands[:, w_low, g_band + i, dx, :], start=n == 0, stop=n == 8,
                                                    skip_group_check=True)
                            n += 1
                return last

            def qk_taps(b, it, s, banks):
                k = b * TILES + it * 2 + s
                for q in banks:
                    pe.wait_ge(qk_split, k * BANKS_T + q + 1)
                    taps(acc[(s * BANKS_T + q) % 4], y2[s], q * GPB, q * GPB).then_inc(tile_full, 1)

            def gram_tile(b, it, s, n_rows):
                k = b * TILES + it * 2 + s
                pe.wait_ge(qk_split, 4 + k * BANKS_T + BANKS_T)
                for r in range(n_rows):
                    for h in range(HEADS):
                        at = (h % 2) * 2 * HQK
                        last = nc.tensor.matmul(gram[h // 2][0:HQK, at:at + 2 * HQK], qk[:, r, 0, h * HQK:(h + 1) * HQK],
                                                qk[:, r, :, h * HQK:(h + 1) * HQK], start=False, stop=False,
                                                skip_group_check=True)
                last.then_inc(gram_tiles, 1)

            def tile(b, it, s, opening):
                pe.wait_ge(y2_loaded[s], (b * ITERS + it + 1) * 16)
                qk_taps(b, it, s, range(2))
                if not opening:
                    gram_tile(b, it - (1 - s), 1 - s, TOUT)
                qk_taps(b, it, s, range(2, BANKS_T))

            def gram_edge(first):
                for g in gram:
                    for i in range(QK // P):
                        last = nc.tensor.matmul(g[0:HQK, i * P:(i + 1) * P], zeros[:, 0:HQK], zeros[:, :],
                                                start=first and i == 0, stop=not first, skip_group_check=True)
                return last

            def value_taps(b, it, s, q):
                k = b * TILES + it * 2 + s
                if q == 0:
                    pe.wait_ge(v_loaded[s], (b * ITERS + it + 1) * 16)
                pe.wait_ge(v_split, k * BANKS_V + q + 1)
                taps(acc[(s * BANKS_V + q) % 2], y2v[s], q * GPB, TG + q * GPB).then_inc(v_full, 1)

            def transpose_pair(b, it, s, rp):
                k = b * TILES + it * 2 + s
                if rp == 0:
                    pe.wait_ge(v_split, 2 + k * BANKS_V + BANKS_V)
                pe.wait_ge(t_copied, k * PAIRS_T + rp + 1)
                for i in range(2):
                    for m in range(3):
                        last = nc.tensor.transpose(tbank[:, (i * 3 + m) * P:(i * 3 + m + 1) * P],
                                                   vrow[:, 2 * rp + i, m * P:(m + 1) * P], ident16[:, :])
                last.then_inc(t_full, 1)

            def output_pair(b, it, s, rp):
                k = b * TILES + it * 2 + s
                pe.wait_ge(t_copied, 1 + k * PAIRS_T + rp + 1)
                pe.wait_ge(z_copied, pair_of(b, it, s, rp) + 1)
                for i in range(2):
                    r = 2 * rp + i
                    out_ps = z_bank(s, rp)[:, i * C:(i + 1) * C]
                    for n, (blk, low, wblk) in enumerate(PRODUCTS):
                        nc.tensor.matmul(out_ps, vt[:, r, blk * P:(blk + 1) * P], m16[:, low, wblk, :], start=n == 0,
                                         stop=False, skip_group_check=True)
                    for blk, wblk in ((0, 0), (1, 0), (2, 1)):
                        row = (xa_hi, xa_lo, xb)[blk][:, bass.ds((it * 2 + s) * TOUT + r, 1), :].rearrange("p a w -> p (a w)")
                        last = nc.tensor.matmul(out_ps, row, eye16[:, wblk, :], start=False, stop=blk == 2,
                                                skip_group_check=True)
                last.then_inc(acc_full, 1)

            def stats_sums(n):
                pe.wait_ge(st_col, n)
                for s in range(2):
                    for i, g in enumerate((grp_a, grp_b)):
                        nc.tensor.matmul(misc[0][:, s * C:(s + 1) * C], colb[:, i, s, :], g[:, 0:C],
                                         start=i == 0, stop=i == 1, skip_group_check=True)
                for m in range(2):
                    for i, g in enumerate((grp_a, grp_b)):
                        last = nc.tensor.matmul(misc[1][:, 2 * m:2 * m + 2], g[:, m * P:(m + 1) * P], col[:, i, :],
                                                start=i == 0, stop=i == 1, skip_group_check=True)
                last.then_inc(st_ps, 1)

            def attention(b):
                pe.wait_ge(gram_copied, 2 + b * 2 + 2)
                pe.wait_ge(zsum_read, 1 + b)
                for h in range(HEADS):
                    last = nc.tensor.transpose(misc[0][0:HQK, h * HQK:(h + 1) * HQK], gs[:, h, HQK:2 * HQK],
                                               ident[0:HQK, 0:HQK])
                last.then_inc(gram_t, 1)
                pe.wait_ge(diag_made, b + 1)
                nc.tensor.matmul(misc[1][0:HQK, 0:QK], ones[0:HQK, 0:HQK], gt.rearrange("p h c -> p (h c)"),
                                 start=True, stop=True).then_inc(colsum, 1)
                value_taps(b, 0, 0, 0)
                pe.wait_ge(attn_loaded, 32 * (b + 1))
                pe.wait_ge(attn_made, b + 1)
                settled(pe)
                for h in range(HEADS):
                    last = nc.tensor.matmul(misc[h // 2][0:HC, (h % 2) * C:(h % 2 + 1) * C], attn[:, h, :], wpt[:, h, :],
                                            start=True, stop=True, skip_group_check=True)
                last.then_inc(mt_ps, 1)
                value_taps(b, 0, 0, 1)
                pe.wait_ge(mt_made, b + 1)
                for i in range(2):
                    for h in range(HEADS):
                        last = nc.tensor.matmul(misc[0][:, i * C:(i + 1) * C], select[:, h, i, :], mt[:, h, :],
                                                start=h == 0, stop=h == HEADS - 1, skip_group_check=True)
                last.then_inc(m_full, 1)

            def image(b, ahead):
                pe.wait_ge(z_copied, 2 + b * (H // 2))
                pe.wait_ge(y_split, 3 + (b + 1) * LOADS * NB)
                gram_edge(True)
                tile(b, 0, 0, True)
                tile(b, 0, 1, False)
                with pe.Fori(1, ITERS) as it:
                    tile(b, it, 0, False)
                    tile(b, it, 1, False)
                gram_tile(b, ITERS - 1, 1, H - (TILES - 1) * TOUT)
                gram_edge(False).then_inc(gram_closed, 1)
                attention(b)
                pe.wait_ge(m_split, b + 1)
                if ahead:
                    stats_sums(b + 2)
                    pe.wait_ge(st_read, b + 2)
                settled(pe)

                def body(it, first, last):
                    norm = ahead and not first
                    for q in range(AHEAD if first else 0, BANKS_V):
                        value_taps(b, it, 0, q)
                    for rp in range(PAIRS_T):
                        if norm:
                            pointwise(b + 1, it - 1, 0, BEFORE_PAIR[rp])
                        transpose_pair(b, it, 0, rp)
                    for q in range(BANKS_V):
                        value_taps(b, it, 1, q)
                    if norm:
                        pointwise(b + 1, it - 1, 1)
                    for rp in range(PAIRS_T):
                        output_pair(b, it, 0, rp)
                    for rp in range(PAIRS_T):
                        if norm:
                            pointwise(b + 1, it - 1, 2, BEFORE_PAIR[rp])
                        transpose_pair(b, it, 1, rp)
                    for rp in range(pairs_in(1, last)):
                        output_pair(b, it, 1, rp)

                loop(pe, body)
                if ahead:
                    for i in range(LAST_LOADS):
                        pointwise(b + 1, ITERS - 1, i)
                pe.wait_ge(z_summed, PAIRS_T + b * (H // 2) + H // 2)
                pe.wait_ge(t_copied, 1 + (b + 1) * TILES * PAIRS_T)
                if ahead:
                    pe.wait_ge(y_split, 3 + (b + 2) * LOADS * NB)
                nc.tensor.matmul(misc[0][:, 0:2 * C], ones[:, :], sum_z, start=True, stop=True)
                nc.tensor.matmul(misc[1][:, 0:2 * C], ones[:, :], sum_q, start=True, stop=True).then_inc(zsum_ps, 1)

            tbank = misc[0][:, :].bitcast(f16)
            pe.wait_ge(const_loaded, 16 * N_CONST)
            pe.wait_ge(consts_made, 1)
            pe.wait_ge(pads_zero, 3)
            pe.wait_ge(w1_made, 1)
            stats_sums(1)
            pe.wait_ge(st_read, 1)
            with pe.Fori(0, ITERS - 1) as it:
                for i in range(PER):
                    pointwise(0, it, i)
            for i in range(LAST_LOADS):
                pointwise(0, ITERS - 1, i)
            pe.wait_ge(bands_made, 1)
            with pe.Fori(0, B - 1) as b:
                image(b, True)
            image(B - 1, False)

        @block.vector
        def _(dve):
            chain = [0, 0]
            LINKS = 33

            def link(ins):
                chain[1] += 1
                ins.then_inc(step_v, 1)
                dve.wait_ge(step_v, chain[0] + chain[1])

            dve.wait_ge(const_loaded, 16 * N_CONST)
            for free, n in ((qk_split, 4), (z_copied, 2), (gram_tiles, 1), (stats_used, 2), (normed, 2), (gram_copied, 2),
                            (zsum_ps, 1), (zsum_read, 1), (z_summed, PAIRS_T), (z_split, PAIRS_T), (z_stored, 16),
                            (y_split, 3), (tile_full, 2 * BANKS_T), (v_full, 2 * BANKS_V), (v_split, 2),
                            (t_full, 1), (t_copied, 1), *((s, 16) for s in y_stored)):
                dve.sem_inc(free, n)
            link(nc.vector.memset(mv[:, :, :], 0.0))
            for w, o0, o1 in ((stage[:, 1, :, 0:QK], 0, QK), (wv_tmp, QK, 3 * C)):
                link(nc.vector.tensor_scalar(w, w, UP, None, ALU.mult))
                link(nc.vector.tensor_copy(w1[:, 0, :, o0:o1], w))
                link(nc.vector.tensor_tensor(w1[:, 1, :, o0:o1], w, w1[:, 0, :, o0:o1], ALU.subtract))
            dve.sem_inc(w1_made, 1)
            for part in range(2):
                src = wide_tmp[:, part, :].rearrange("p (n c) -> p n c", c=1).to_broadcast([HQK, PIECES, PIECE])
                for a in range(2):
                    hi, lo = [table[:, part, s, a * W:(a + 1) * W].rearrange("p (n c) -> p n c", c=PIECE) for s in range(2)]
                    link(nc.vector.tensor_copy(hi, src))
                    link(nc.vector.tensor_tensor(lo, src, hi, ALU.subtract))
                dve.sem_inc(table_made, 1)

            def arrived(b, it, i, per_load, before):
                slot = SLOTS[i]
                n = it * SLOTS.count(slot) + SLOTS[:i].count(slot) + 1
                return 16 * (b * IN_SLOT[slot] * 5 - (1 - before) * IN_SLOT[slot] * 2 + per_load * n)

            def stats_load(b, it, i):
                slot, n = SLOTS[i], it * PER + i
                dve.wait_ge(loaded[slot], arrived(b, it, i, 2, 0))
                nc.vector.bn_stats(stats[:, 0, bass.ds(n, 1), :].rearrange("p a s -> p (a s)"), stage[:, slot, 0, :])
                nc.vector.bn_stats(stats[0:CB, 1, bass.ds(n, 1), :].rearrange("p a s -> p (a s)"), stage[0:CB, slot, 1, :])\
                    .then_inc(stats_used, 1)

            def stats_final(b, turn):
                dve.wait_ge(stats_used, 2 + b * LOADS + LOADS)
                settled(dve)
                nc.vector.bn_aggr(mv[:, 0, :], stats[:, 0, :, :].rearrange("p n s -> p (n s)"))
                link(nc.vector.bn_aggr(mv[0:CB, 1, :], stats[0:CB, 1, :, :].rearrange("p n s -> p (n s)")))
                nc.vector.tensor_copy(col[:, :, 0], mv[:, :, 0])
                link(nc.vector.tensor_tensor(col[:, :, 1], mv[:, :, 0], mv[:, :, 0], ALU.mult))
                link(nc.vector.tensor_tensor(col[:, :, 1], col[:, :, 1], mv[:, :, 1], ALU.add))
                nc.vector.tensor_copy(colb[:, :, :, :], col[:, :, :].rearrange("p i (s a) -> p i s a", a=1)
                                      .to_broadcast([P, 2, 2, P])).then_inc(st_col, 1)
                dve.wait_ge(st_ps, b + 1)
                sums = misc[0][:, 0:2 * C].rearrange("p (s g c) -> p s g c", s=2, c=GC)
                nc.vector.tensor_copy(st_m[:, 0:GROUPS], sums[:, 0, :, 0])
                nc.vector.tensor_copy(st_v[:, 0:GROUPS], sums[:, 1, :, 0])
                nc.vector.tensor_copy(st_m[:, GROUPS:], misc[1][:, 0:4:2])
                nc.vector.tensor_copy(st_v[:, GROUPS:], misc[1][:, 1:4:2]).then_inc(st_read, 1)
                dve.wait_ge(st_read, b + 1)
                link(nc.vector.tensor_tensor(st_t[:, :], st_m[:, :], st_m[:, :], ALU.mult))
                link(nc.vector.tensor_tensor(st_v[:, :], st_v[:, :], st_t[:, :], ALU.subtract))
                nc.vector.tensor_scalar(st_v[:, :], st_v[:, :], 0.0, EPS, ALU.max, ALU.add).then_inc(var_made, 1)
                dve.wait_ge(sd_made, turn)
                nc.vector.tensor_copy(t_sd[:, bass.ds(b, 1), :].rearrange("p a g -> p (a g)"), st_t[:, 0:GROUPS])
                nc.vector.tensor_copy(t_mean[:, bass.ds(b, 1), :].rearrange("p a g -> p (a g)"), st_m[:, 0:GROUPS])
                link(nc.vector.reciprocal(st_v[:, :], st_t[:, :]))
                nc.vector.tensor_copy(st_scale[:, :], st_v[:, GROUPS:])
                nc.vector.scalar_tensor_tensor(nbias[:, :], st_m[:, GROUPS:], -1.0, st_v[:, GROUPS:], ALU.mult, ALU.mult)
                link(nc.vector.tensor_scalar(r0up[:, :].rearrange("p (g c) -> p g c", c=GC),
                                             st_v[:, 0:GROUPS].rearrange("p (g a) -> p g a", a=1).to_broadcast([P, GROUPS, GC]),
                                             UP, None, ALU.mult))

            def normalise_scale(b, it, i):
                slot = SLOTS[i]
                dve.wait_ge(loaded[slot], arrived(b, it, i, 3, 1))
                for k in range(2):
                    nc.vector.tensor_scalar(stage[:, slot, k, :], stage[:, slot, k, :], st_scale[:, k:k + 1],
                                            nbias[:, k:k + 1], ALU.mult, ALU.add).then_inc(affine, 1)

            def normalise_lo(b, it, i):
                slot, n = SLOTS[i], it * PER + i
                dve.wait_ge(hi_made, (b * LOADS + n) * 3 + 3)
                nc.vector.tensor_tensor(quad_rows(1, n), rows(stage[:, slot, 0, :]), quad_rows(0, n), ALU.subtract)
                nc.vector.tensor_tensor(quad_rows(2, n)[CB:P], rows(stage[CB:P, slot, 1, :]), rows(stage_hi[CB:P, :]),
                                        ALU.subtract).then_inc(normed, 1)

            def y_low(b, it, i, blocks=range(NB)):
                for t in blocks:
                    m = BLOCKS[t][1] - BLOCKS[t][0]
                    dve.wait_ge(y_hi, unit(b, it, i, t) + 1)
                    nc.vector.tensor_tensor(ystage[0:m, t, :, 1, 1:1 + W], rows(y_bank(i, t)[0:m, :]),
                                            ystage[0:m, t, :, 0, 1:1 + W], ALU.subtract).then_inc(y_split, 1)

            def step(b, it, i, it2, i2):
                normalise_scale(b, it2, i2)
                y_low(b, it, i, range(0, 3))
                normalise_lo(b, it2, i2)
                y_low(b, it, i, range(3, NB))

            def value_low(b, it, s, q):
                dve.wait_ge(v_hi, (b * TILES + it * 2 + s) * BANKS_V + q + 1)
                nc.vector.tensor_tensor(value_out(q, 1), value_in(s, q), value_out(q, 0), ALU.subtract).then_inc(v_split, 1)

            def copy_transposed(b, it, s, rp):
                dve.wait_ge(t_full, 1 + (b * TILES + it * 2 + s) * PAIRS_T + rp + 1)
                nc.vector.tensor_copy(vt[:, 2 * rp:2 * rp + 2, :].rearrange("p r c -> p (r c)"),
                                      misc[0][:, :].bitcast(f16)[:, 0:6 * P]).then_inc(t_copied, 1)

            def z_low(b, it, s, rp):
                dve.wait_ge(z_copied, 2 + pair_of(b, it, s, rp) + 1)
                hi, lo = [z_out[:, :, 2 * rp:2 * rp + 2, half, :].rearrange("p g r c -> p r g c") for half in range(2)]
                nc.vector.tensor_tensor(lo, zf[:, rp, :].rearrange("p (r g c) -> p r g c", r=2, c=CG), hi, ALU.subtract)\
                    .then_inc(z_split, 1)

            def attention(b):
                dve.wait_ge(gram_closed, b + 1)
                for g in range(2):
                    nc.vector.tensor_copy(gs[:, 2 * g:2 * g + 2, :], gram[g][0:HQK, 0:QK].rearrange("p (h c) -> p h c", h=2))\
                        .then_inc(gram_copied, 1)
                dve.wait_ge(gram_t, b + 1)
                dve.wait_ge(gram_copied, 2 + b * 2 + 2)
                link(nc.vector.tensor_tensor(gg[:, :, :], gs[:, :, 0:HQK], gs[:, :, HQK:2 * HQK], ALU.add))
                link(nc.vector.tensor_tensor(gg[:, :, :], misc[0][0:HQK, 0:QK].rearrange("p (h c) -> p h c", h=HEADS),
                                             gg[:, :, :], ALU.add))
                eye = ident[0:HQK, 0:HQK].rearrange("p (a c) -> p a c", a=1).to_broadcast([HQK, HEADS, HQK])
                nc.vector.tensor_tensor(gt[:, :, :], gg[:, :, :], eye, ALU.mult).then_inc(diag_made, 1)
                dve.wait_ge(diag_made, b + 1)
                link(nc.vector.tensor_reduce(small[:, :], gt[0:HC, :, 0:HC], AX.X, ALU.add))
                nc.vector.tensor_scalar(small[:, :], small[:, :], 0.0, None, ALU.max).then_inc(norms_ready, 1)
                dve.wait_ge(colsum, b + 1)
                nc.vector.tensor_scalar(gt[0:HC, :, HC:HQK],
                                        misc[1][0:HC, 0:QK].rearrange("p (h c) -> p h c", h=HEADS)[:, :, HC:HQK],
                                        0.0, None, ALU.max).then_inc(norms_ready, 1)
                dve.wait_ge(norms_rooted, b * 2 + 2)
                link(nc.vector.tensor_scalar(kn[:, :, :], kn[:, :, :], NORM_EPS * UP, None, ALU.max))
                link(nc.vector.tensor_scalar(qn[:, :], qn[:, :], NORM_EPS * UP, None, ALU.max))
                link(nc.vector.reciprocal(kn[:, :, :], kn[:, :, :]))
                link(nc.vector.reciprocal(qn[:, :], qn[:, :]))
                link(nc.vector.tensor_tensor(qn[:, :], qn[:, :], temp[:, :], ALU.mult))
                link(nc.vector.tensor_tensor(attn[:, :, :], gg[0:HC, :, HC:HQK], kn[:, :, :], ALU.mult))

                def over(t):
                    return t[:, :].rearrange("p (h a) -> p h a", a=1).to_broadcast([HC, HEADS, HC])

                link(nc.vector.tensor_tensor(attn[:, :, :], attn[:, :, :], over(qn), ALU.mult))
                link(nc.vector.tensor_reduce(small[:, :], attn[:, :, :], AX.X, ALU.max))
                nc.vector.tensor_tensor(attn[:, :, :], attn[:, :, :], over(small), ALU.subtract).then_inc(logits, 1)
                dve.wait_ge(exped, b + 1)
                link(nc.vector.tensor_reduce(small[:, :], gt[0:HC, :, 0:HC], AX.X, ALU.add))
                link(nc.vector.reciprocal(small[:, :], small[:, :]))
                nc.vector.tensor_tensor(attn[:, :, :], gt[0:HC, :, 0:HC], over(small), ALU.mult).then_inc(attn_made, 1)
                dve.wait_ge(mt_ps, b + 1)
                for g in range(2):
                    link(nc.vector.tensor_tensor(mt[:, 2 * g:2 * g + 2, :],
                                                 misc[g][0:HC, 0:2 * C].rearrange("p (h c) -> p h c", h=2),
                                                 r0up[0:HC, :].rearrange("p (a c) -> p a c", a=1).to_broadcast([HC, 2, C]),
                                                 ALU.mult))

                dve.sem_inc(mt_made, 1)
                dve.wait_ge(m_hi, b + 1)
                nc.vector.tensor_tensor(m16[:, 1, :, :], misc[0][:, 0:2 * C].rearrange("p (i c) -> p i c", i=2),
                                        m16[:, 0, :, :], ALU.subtract).then_inc(m_split, 1)

            def z_final(b, ahead):
                dve.wait_ge(zsum_ps, 1 + b + 1)
                dve.wait_ge(sd_made, b * 2 + 2 if ahead else b * 2 + 1)
                for i, t in enumerate((st_m, st_v)):
                    link(nc.vector.tensor_reduce(t[:, 0:GROUPS],
                                                 misc[i][:, 0:2 * C].rearrange("p (r g c) -> p g r c", r=2, c=GC),
                                                 AX.XY, ALU.add))
                dve.sem_inc(zsum_read, 1)
                link(nc.vector.tensor_scalar(st_v[:, 0:GROUPS], st_v[:, 0:GROUPS], 1.0 / N_GROUP, None, ALU.mult))
                link(nc.vector.tensor_scalar(st_m[:, 0:GROUPS], st_m[:, 0:GROUPS], 1.0 / N_GROUP, None, ALU.mult))
                sd0 = t_sd[:, bass.ds(b, 1), :].rearrange("p a g -> p (a g)")
                link(nc.vector.tensor_tensor(st_t[:, 0:GROUPS], st_m[:, 0:GROUPS], st_m[:, 0:GROUPS], ALU.mult))
                link(nc.vector.tensor_tensor(st_v[:, 0:GROUPS], st_v[:, 0:GROUPS], st_t[:, 0:GROUPS], ALU.subtract))
                link(nc.vector.tensor_tensor(st_v[:, 0:GROUPS], st_v[:, 0:GROUPS], sd0, ALU.mult))
                link(nc.vector.tensor_tensor(st_v[:, 0:GROUPS], st_v[:, 0:GROUPS], sd0, ALU.mult))
                nc.vector.tensor_scalar(st_v[:, 0:GROUPS], st_v[:, 0:GROUPS], 0.0, EPS, ALU.max, ALU.add).then_inc(var_made, 1)
                dve.wait_ge(sd_made, b * 2 + 3 if ahead else b * 2 + 2)
                link(nc.vector.reciprocal(st_v[:, 0:GROUPS], st_t[:, 0:GROUPS]))
                s1 = t_s1[:, bass.ds(b, 1), :].rearrange("p a g -> p (a g)")
                link(nc.vector.tensor_tensor(s1, st_v[:, 0:GROUPS], sd0, ALU.mult))
                link(nc.vector.tensor_tensor(t_s1m[:, bass.ds(b, 1), :].rearrange("p a g -> p (a g)"), s1,
                                             st_m[:, 0:GROUPS], ALU.mult))

            def image(b, ahead):
                def tiles(it, n_stats):
                    done = 0
                    for s in range(2):
                        k = b * TILES + it * 2 + s
                        for q in range(BANKS_T):
                            dve.wait_ge(qk_hi, k * BANKS_T + q + 1)
                            nc.vector.tensor_tensor(tile_out(q, 1), tile_in(s, q), tile_out(q, 0), ALU.subtract)\
                                .then_inc(qk_split, 1)
                            if ahead and (s * BANKS_T + q) % 4 == 3 and done < n_stats:
                                stats_load(b + 1, it, done)
                                done += 1

                with dve.Fori(0, ITERS - 1) as it:
                    tiles(it, PER)
                tiles(ITERS - 1, LAST_LOADS)
                attention(b)
                if ahead:
                    stats_final(b + 1, b * 2 + 2)

                def body(it, first, last):
                    norm = ahead and not first
                    for q in range(BANKS_V):
                        value_low(b, it, 0, q)
                        if norm and q == 0:
                            normalise_lo(b + 1, it - 1, 0)
                    if norm:
                        normalise_scale(b + 1, it - 1, 1)
                        y_low(b + 1, it - 1, 0, range(0, 2))
                    for rp in range(PAIRS_T):
                        copy_transposed(b, it, 0, rp)
                        if norm:
                            y_low(b + 1, it - 1, 0, range(2 + rp, 3 + rp))
                    for q in range(BANKS_V):
                        value_low(b, it, 1, q)
                        if norm and q == 0:
                            normalise_lo(b + 1, it - 1, 1)
                    if norm:
                        normalise_scale(b + 1, it - 1, 2)
                        y_low(b + 1, it - 1, 1)
                        normalise_lo(b + 1, it - 1, 2)
                    for rp in range(PAIRS_T):
                        z_low(b, it, 0, rp)
                    if norm:
                        y_low(b + 1, it - 1, 2, range(0, 2))
                    for rp in range(PAIRS_T):
                        copy_transposed(b, it, 1, rp)
                        if norm:
                            y_low(b + 1, it - 1, 2, range(2 + rp, 3 + rp))
                    if ahead:
                        normalise_scale(b + 1, it, 0)
                    for rp in range(pairs_in(1, last)):
                        z_low(b, it, 1, rp)

                loop(dve, body)
                if ahead:
                    normalise_lo(b + 1, ITERS - 1, 0)
                    step(b + 1, ITERS - 1, 0, ITERS - 1, 1)
                    y_low(b + 1, ITERS - 1, 1)
                z_final(b, ahead)

            with dve.Fori(0, H // (FIRST_SLOTS * FIRST_ROWS)) as j:
                for slot in range(FIRST_SLOTS):
                    dve.wait_ge(first_loaded[slot], (j + 1) * 32)
                    for half in range(FIRST_ROWS // LOAD_ROWS):
                        n = (j * FIRST_SLOTS + slot) * (FIRST_ROWS // LOAD_ROWS) + half
                        at = slice(half * NLOAD, (half + 1) * NLOAD)
                        nc.vector.bn_stats(stats[:, 0, bass.ds(n, 1), :].rearrange("p a s -> p (a s)"),
                                           first_rows[:, slot, 0, at])
                        nc.vector.bn_stats(stats[0:CB, 1, bass.ds(n, 1), :].rearrange("p a s -> p (a s)"),
                                           first_rows[0:CB, slot, 1, at]).then_inc(stats_used, 1)
            stats_final(0, 1)
            normalise_scale(0, 0, 0)
            normalise_lo(0, 0, 0)
            with dve.Fori(0, ITERS - 1) as it:
                for i in range(PER):
                    step(0, it, i, it + (i + 1) // PER, (i + 1) % PER)
            step(0, ITERS - 1, 0, ITERS - 1, 1)
            y_low(0, ITERS - 1, 1)
            base = chain[1]
            with dve.Fori(0, B - 1) as b:
                chain[1] = 0
                chain[0] = b * LINKS + base
                image(b, True)
                assert chain[1] == LINKS, chain[1]
            chain[0] = (B - 1) * LINKS + base
            chain[1] = 0
            image(B - 1, False)

        layer0_block.close()
        layer0.close()
        stack.pop()
        layer1 = ctx.enter_context(ExitStack())
        stack.append(layer1)
        wide = sb("wide", [P, 2, CG, 2, W], f16)
        zin = sb("zin", [P, 2, H, 2, CG], f16)
        mixed_out = sb("mixed_out", [P, 2, CG, W])
        shift = sb("shift", [P, B, C])
        wsum = sb("wsum", [P, C])
        wsum_in = sb("wsum_in", [PIECES, C])
        bias_row = sb("bias_row", [P, C])
        held = sb("held", [PIECES, P])

        b_in = sem("b_in")
        held_made = sem("held_made")
        wsum_ps = sem("wsum_ps")
        shift_step = sem("shift_step")
        wide_in = [sem("wide_in0"), sem("wide_in1")]
        z_in = [sem("z_in0"), sem("z_in1")]
        quad_full = sem("quad_full")
        shifted = sem("shifted")
        quad_out = sem("quad_out")
        stored = sem("stored")
        out_free = sem("out_free")

        block1 = ctx.enter_context(nc.Block())

        @block1.sync
        def _(sp):
            sp.dma_start(wsum_in[:, :], wide_t).then_inc(b_in, 16)
            sp.dma_start(bias_row[:, :], bias.rearrange("(a c) -> a c", a=1).to_broadcast([P, C])).then_inc(b_in, 16)
            sp.wait_ge(held_made, 1)

            def load_wide(g):
                if g >= 2:
                    sp.wait_ge(quad_full, 2 * QUADS + (g - 1) * B * QUADS)
                sp.dma_start(wide[:, g % 2, :, :, :],
                             bass.AP(tensor=tab_dram.tensor, offset=g * CG * 4 * W + 1,
                                     ap=[[1, P], [4 * W, CG], [2 * W, 2], [1, W]])).then_inc(wide_in[g % 2], 16)

            def load_z(g, i):
                for s in range(2):
                    sp.wait_ge(quad_full, (g * B + i * 2 + s) * QUADS + QUADS)
                    sp.dma_start(zin[:, s, :, :, :].rearrange("p h s c -> p (h s c)"),
                                 z_dram[bass.ds(i * 2 + s, 1), :, g, :, :, :]
                                 .rearrange("b p h s c -> p (b h s c)")).then_inc(z_in[s], 16)

            load_wide(0)
            for g in range(CGROUPS):
                load_z(g, 0)
                if g + 1 < CGROUPS:
                    load_wide(g + 1)
                with sp.Fori(1, B // 2) as i:
                    load_z(g, i)

        @block1.gpsimd
        def _(pool):
            nc.gpsimd.memset(held[:, :], float(PIECE)).then_inc(held_made, 1)
            with pool.Fori(0, CGROUPS) as g:
                with pool.Fori(0, B // 2) as i:
                    for s in range(2):
                        pool.wait_ge(quad_out, 3 + (g * B + i * 2 + s) * QUADS + QUADS)
                        pool.dma_start(out[bass.ds(i * 2 + s, 1), bass.ds(g * CG, CG), :, :].rearrange("b c h w -> h (b c) w"),
                                       mixed_out[:, s, :, :]).then_inc(stored, 16)
                        pool.wait_ge(stored, (g * B + i * 2 + s + 1) * 16)
                        pool.sem_inc(out_free, 1)
            pool.wait_ge(stored, 16 * CGROUPS * B)

        @block1.tensor
        def _(pe):
            pe.sem_inc(quad_full, 2 * QUADS)
            pe.wait_ge(b_in, 32)
            pe.wait_ge(held_made, 1)
            nc.tensor.matmul(psum[7][:, 0:C], held[:, :], wsum_in[:, :], start=True, stop=True).then_inc(wsum_ps, 1)
            with pe.Fori(0, CGROUPS // 2) as gp:
                for gs_ in range(2):
                    pe.wait_ge(wide_in[gs_], (gp + 1) * 16)
                    pe.sem_inc(carried, 1)
                    with pe.Fori(0, B // 2) as i:
                        for s in range(2):
                            step = gp * (2 * B) + gs_ * B + i * 2 + s
                            pe.wait_ge(z_in[s], (gp * B + gs_ * (B // 2) + i + 1) * 16)
                            for q in range(QUADS):
                                pe.wait_ge(quad_out, step * QUADS + q + 1)
                                for k in range(QUAD):
                                    c = q * QUAD + k
                                    z_hi, z_lo = zin[:, s, :, 0, c], zin[:, s, :, 1, c]
                                    w_hi, w_lo = wide[:, gs_, c, 0, ::-1], wide[:, gs_, c, 1, ::-1]
                                    conv = psum[q % 3][:, k * W:(k + 1) * W]
                                    res = psum[3 + q % 3][:, k * W:(k + 1) * W]
                                    nc.tensor.matmul(conv, z_hi, w_hi, start=True, stop=False, skip_group_check=True)
                                    nc.tensor.matmul(conv, z_hi, w_lo, start=False, stop=False, skip_group_check=True)
                                    nc.tensor.matmul(res, z_hi, ident16[:, :], start=True, stop=False, skip_group_check=True)
                                    nc.tensor.matmul(conv, z_lo, w_hi, start=False, stop=True, skip_group_check=True)
                                    last = nc.tensor.matmul(res, z_lo, ident16[:, :], start=False, stop=True,
                                                            skip_group_check=True)
                                last.then_inc(quad_full, 1)

        @block1.scalar
        def _(act):
            act.wait_ge(shift_step, 1 + 3 * B)
            with act.Fori(0, CGROUPS) as g:
                with act.Fori(0, B // 2) as i:
                    for s in range(2):
                        step = g * B + i * 2 + s
                        act.wait_ge(out_free, step + 1)
                        sd = t_sd[:, bass.ds(i * 2 + s, 1), :].rearrange("p a g -> p (a g)")[:, bass.ds(g * (CG // GC), CG // GC)]
                        sh = shift[:, bass.ds(i * 2 + s, 1), :].rearrange("p a c -> p (a c)")[:, bass.ds(g * CG, CG)]
                        for q in range(QUADS):
                            act.wait_ge(quad_full, step * QUADS + 2 * QUADS + q + 1)
                            for k in range(QUAD):
                                c = q * QUAD + k
                                last = nc.scalar.activation(mixed_out[:, s, c, :], psum[3 + q % 3][:, k * W:(k + 1) * W],
                                                            ACT.Identity, scale=sd[:, c // GC:c // GC + 1],
                                                            bias=sh[:, c:c + 1])
                            last.then_inc(shifted, 1)

        @block1.vector
        def _(dve):
            dve.sem_inc(quad_out, 3)
            dve.sem_inc(out_free, 2)
            dve.wait_ge(wsum_ps, 1)
            nc.vector.tensor_copy(wsum[:, :], psum[7][:, 0:C]).then_inc(shift_step, 1)
            for b in range(B):
                def wide_row(t):
                    return t[:, b, :].rearrange("p (g a) -> p g a", a=1).to_broadcast([P, GROUPS, GC])

                row = shift[:, b, :].rearrange("p (g c) -> p g c", c=GC)
                dve.wait_ge(shift_step, 1 + 3 * b)
                nc.vector.tensor_tensor(row, wsum[:, :].rearrange("p (g c) -> p g c", c=GC), wide_row(t_s1m), ALU.mult)\
                    .then_inc(shift_step, 1)
                dve.wait_ge(shift_step, 2 + 3 * b)
                nc.vector.tensor_tensor(row, wide_row(t_mean), row, ALU.subtract).then_inc(shift_step, 1)
                dve.wait_ge(shift_step, 3 + 3 * b)
                nc.vector.tensor_tensor(shift[:, b, :], shift[:, b, :], bias_row[:, :], ALU.add).then_inc(shift_step, 1)
            with dve.Fori(0, CGROUPS) as g:
                with dve.Fori(0, B // 2) as i:
                    for s in range(2):
                        step = g * B + i * 2 + s
                        sc = t_s1[:, bass.ds(i * 2 + s, 1), :].rearrange("p a g -> p (a g)")[:, bass.ds(g * (CG // GC), CG // GC)]
                        for q in range(QUADS):
                            dve.wait_ge(shifted, step * QUADS + q + 1)
                            for k in range(QUAD):
                                c = q * QUAD + k
                                last = nc.vector.scalar_tensor_tensor(mixed_out[:, s, c, :], psum[q % 3][:, k * W:(k + 1) * W],
                                                                      sc[:, c // GC:c // GC + 1], mixed_out[:, s, c, :],
                                                                      ALU.mult, ALU.add)
                            last.then_inc(quad_out, 1)


def kernel(**inputs):
    import numpy as np
    import concourse.bacc as bacc
    from concourse import mybir
    from concourse.bass_utils import run_bass_kernel_spmd

    a = {k: np.asarray(v) for k, v in inputs.items()}
    order = np.concatenate([np.concatenate([np.arange(h * HC, (h + 1) * HC), C + np.arange(h * HC, (h + 1) * HC)])
                            for h in range(HEADS)])
    w_qkv, w_dw = a["L0_conv_w_qkv"], a["L0_conv_w_dw"].reshape(3 * C, TAPS)
    wide = a["L1_conv_weights"].reshape(C, PIECES)
    ch = np.arange(C)
    same = (ch[:, None] // GC == ch[None, :] // GC).astype(np.float32)
    cols = np.concatenate([ch[:CA], ch[CA:], ch[CA:]])
    p, n, d = np.arange(P)[:, None, None], np.arange(BAND)[None, None, :], np.arange(3)[None, :, None]
    masks = ((p % TC == n % TC) & (p // TC - n // TC == d)).astype(np.float32)
    select = np.zeros((HC, HEADS, 2, P), np.float32)
    for d in range(C):
        c, g = divmod(d, GV)
        if g < GVA:
            select[d % HC, d // HC, 0, c * GVA + g] = 1
        else:
            for half in range(2):
                select[d % HC, d // HC, 1, half * CB + c * (GV - GVA) + g - GVA] = 1
    select = select.reshape(HC, -1)
    arrays = {
        "x": a["x"],
        "w_qk": np.concatenate([w_qkv[order], w_qkv[2 * C:]]).T,
        "w_dw": np.concatenate([w_dw[order].reshape(TC, TG * TAPS), w_dw[2 * C:].reshape(TC, GV * TAPS)], axis=1),
        "masks": masks, "select": select,
        "w_proj_t": a["L0_conv_w_proj"].T, "temperature": a["L0_conv_temperature"].reshape(HEADS),
        "wide_w": wide, "wide_t": wide.T, "bias": a["L1_conv_bias"],
        "group_a": same[:CA][:, cols] / np.float32(GC),
        "group_b": np.concatenate([same[CA:], np.zeros_like(same[CA:])])[:, cols] / np.float32(GC),
        "ident": np.eye(P, dtype=np.float32),
        "res_eye": np.float32(UP ** 2) * np.stack([np.eye(C, dtype=np.float32)[:CA],
                                              np.eye(C, dtype=np.float32)[np.concatenate([ch[CA:], ch[CA:]])]], axis=1),
    }
    nc = bacc.Bacc("TRN2", target_bir_lowering=False, num_devices=1)
    arrays = {f"in_{k}": np.ascontiguousarray(v) for k, v in arrays.items()}
    args = [nc.dram_tensor(k, v.shape, mybir.dt.from_np(v.dtype), kind="ExternalInput").ap() for k, v in arrays.items()]
    out = nc.dram_tensor("out", [B, C, H, W], mybir.dt.float32, kind="ExternalOutput").ap()
    conv_kernel(nc, *args, out)
    result = run_bass_kernel_spmd(nc, [arrays], core_ids=[0])
    return result.results[0]["out"]
```
